# Optimizing a Trainium2 kernel written in Bass

```python
import numpy as np
import jax
import jax.numpy as jnp

def _softmax(x, axis=-1):
    return jax.nn.softmax(x, axis=axis)

def _gelu(x):
    return jax.nn.gelu(x, approximate=True)

def _silu(x):
    return jax.nn.silu(x)

def _sigmoid(x):
    return jax.nn.sigmoid(x)

def _layernorm(x, axis=-1, eps=1e-05):
    m = jnp.mean(x, axis=axis, keepdims=True)
    v = jnp.var(x, axis=axis, keepdims=True)
    return (x - m) / jnp.sqrt(v + eps)

def _scatter_add(tgt, idx, src, axis=0):
    return tgt.at[idx].add(src)

def _segment_sum(src, seg, n):
    return jax.ops.segment_sum(src, seg, n)
kernel_name = 'mk_gnn_preln_d2_gnn_r8_c5a58b'

def setup_inputs(seed: int=0):
    np.random.seed(seed)
    _w = jnp.asarray

    def _rec_inputs():
        import jax
        import jax.numpy as jnp
        _gk = jax.random.key(seed)
        x = -0.0001006 + 1 * jax.random.normal(jax.random.fold_in(_gk, 1), (6250, 96), jnp.float32)
        src = jax.random.randint(jax.random.fold_in(_gk, 2), (100000,), 0, 6250, jnp.int32)
        dst = jax.random.randint(jax.random.fold_in(_gk, 3), (100000,), 0, 6250, jnp.int32)
        _o = jnp.argsort(dst, stable=True)
        src = src[_o]
        dst = dst[_o]
        edge_attr_64 = 0.000189758 + 1.00013 * jax.random.normal(jax.random.fold_in(_gk, 12), (100000, 64), jnp.float32)
        edge_weight = jax.random.uniform(jax.random.fold_in(_gk, 14), (100000,), jnp.float32, 0.0, 0.999998)
        return (x, src, dst, edge_attr_64, edge_weight)
    x, src, dst, edge_attr_64, edge_weight = _rec_inputs()

    def _L0_gnn_setup():
        import jax, jax.numpy as jnp
        import numpy as np
        N, E = (6250, 100000)
        NODE_DIM, EDGE_DIM = (96, 64)
        IN_DIM = 2 * NODE_DIM + EDGE_DIM
        key = jax.random.key(seed)
        k = jax.random.split(key, 7)
        h = jax.random.normal(k[0], (N, NODE_DIM), dtype=jnp.float32)
        edge_index = jax.random.randint(k[1], (2, E), 0, N, dtype=jnp.int64)
        edge_attr = jax.random.normal(k[2], (E, EDGE_DIM), dtype=jnp.float32)
        s = 1.0 / np.sqrt(IN_DIM)
        W_e = jax.random.uniform(k[3], (IN_DIM, NODE_DIM), jnp.float32, -s, s)
        b_e = jax.random.uniform(k[4], (NODE_DIM,), jnp.float32, -s, s)
        W_n = jax.random.uniform(k[5], (IN_DIM, NODE_DIM), jnp.float32, -s, s)
        b_n = jax.random.uniform(k[6], (NODE_DIM,), jnp.float32, -s, s)
        return {'h': h, 'edge_index': edge_index, 'edge_attr': edge_attr, 'W_e': W_e, 'b_e': b_e, 'W_n': W_n, 'b_n': b_n}
    _L0_gnn_all = _L0_gnn_setup()
    _L0_gnn_in = {k: v for k, v in _L0_gnn_all.items() if k in ('W_e', 'b_e', 'W_n', 'b_n')}
    del _L0_gnn_all

    def _L1_gnn_setup():
        import jax, jax.numpy as jnp
        import numpy as np
        N = 6250
        E = 100000
        D = 96

        def gcn_conv(x, row, col, ew, W, b):
            n = x.shape[0]
            h = x @ W
            deg = jax.ops.segment_sum(ew, col, num_segments=n) + 1.0
            dinv = jnp.where(deg > 0, jax.lax.rsqrt(deg), 0.0)
            norm = dinv[row] * ew * dinv[col]
            agg = jax.ops.segment_sum(h[row] * norm[:, None], col, num_segments=n)
            agg = agg + h * (dinv * dinv)[:, None]
            return agg + b
        key = jax.random.key(seed)
        ks = jax.random.split(key, 8)
        x = jax.random.normal(ks[0], (N, D), dtype=jnp.float32)
        edge_index = jax.random.randint(ks[1], (2, E), 0, N, dtype=jnp.int32)
        edge_weight = jax.random.uniform(ks[2], (E,), dtype=jnp.float32)
        batch = jnp.zeros((N,), dtype=jnp.int32)
        s = 1.0 / np.sqrt(D)
        W1 = jax.random.normal(ks[3], (D, D), dtype=jnp.float32) * s
        b1 = jnp.zeros((D,), dtype=jnp.float32)
        W2 = jax.random.normal(ks[4], (D, D), dtype=jnp.float32) * s
        b2 = jnp.zeros((D,), dtype=jnp.float32)
        return {'x': x, 'edge_index': edge_index, 'edge_weight': edge_weight, 'batch': batch, 'W1': W1, 'b1': b1, 'W2': W2, 'b2': b2}
    _L1_gnn_all = _L1_gnn_setup()
    _L1_gnn_in = {k: v for k, v in _L1_gnn_all.items() if k in ('W1', 'b1', 'W2', 'b2')}
    del _L1_gnn_all
    return {'x': x, 'src': src, 'dst': dst, 'edge_attr_64': edge_attr_64, 'edge_weight': edge_weight, 'L0_gnn_W_e': _L0_gnn_in['W_e'], 'L0_gnn_b_e': _L0_gnn_in['b_e'], 'L0_gnn_W_n': _L0_gnn_in['W_n'], 'L0_gnn_b_n': _L0_gnn_in['b_n'], 'L1_gnn_W1': _L1_gnn_in['W1'], 'L1_gnn_b1': _L1_gnn_in['b1'], 'L1_gnn_W2': _L1_gnn_in['W2'], 'L1_gnn_b2': _L1_gnn_in['b2']}

def reference(x, src, dst, edge_attr_64, edge_weight, L0_gnn_W_e, L0_gnn_b_e, L0_gnn_W_n, L0_gnn_b_n, L1_gnn_W1, L1_gnn_b1, L1_gnn_W2, L1_gnn_b2):
    import jax
    import jax.numpy as jnp

    def _L0_gnn_ref(h, edge_index, edge_attr, W_e, b_e, W_n, b_n):
        import jax, jax.numpy as jnp
        import numpy as np
        N, E = (6250, 100000)
        NODE_DIM, EDGE_DIM = (96, 64)
        IN_DIM = 2 * NODE_DIM + EDGE_DIM
        src, dst = (edge_index[0], edge_index[1])
        concat = jnp.concatenate([h[src], h[dst], edge_attr], axis=-1)
        gates = jax.nn.sigmoid(concat @ W_e + b_e)
        messages = jax.nn.softplus(concat @ W_n + b_n)
        gated = gates * messages
        n = h.shape[0]
        h_new = jax.ops.segment_sum(gated, dst, num_segments=n)
        edge_count = jax.ops.segment_sum(jnp.ones((dst.shape[0],), h.dtype), dst, num_segments=n)
        edge_count = jnp.clip(edge_count, 1.0, None)[:, None]
        return h + h_new / edge_count

    def _L1_gnn_ref(x, edge_index, edge_weight, batch, W1, b1, W2, b2):
        import jax, jax.numpy as jnp
        import numpy as np
        N = 6250
        E = 100000
        D = 96

        def gcn_conv(x, row, col, ew, W, b):
            n = x.shape[0]
            h = x @ W
            deg = jax.ops.segment_sum(ew, col, num_segments=n) + 1.0
            dinv = jnp.where(deg > 0, jax.lax.rsqrt(deg), 0.0)
            norm = dinv[row] * ew * dinv[col]
            agg = jax.ops.segment_sum(h[row] * norm[:, None], col, num_segments=n)
            agg = agg + h * (dinv * dinv)[:, None]
            return agg + b
        row, col = (edge_index[0], edge_index[1])
        h = jax.nn.relu(gcn_conv(x, row, col, edge_weight, W1, b1))
        h = jax.nn.relu(gcn_conv(h, row, col, edge_weight, W2, b2))
        return h
    edge_index = jnp.stack([src, dst])
    batch0 = jnp.zeros((6250,), jnp.int32)
    h = jnp.maximum(_layernorm(x, axis=-1), 0.0)
    x = x + _L0_gnn_ref(h, edge_index, edge_attr_64, L0_gnn_W_e, L0_gnn_b_e, L0_gnn_W_n, L0_gnn_b_n)
    h = jnp.maximum(_layernorm(x, axis=-1), 0.0)
    x = x + _L1_gnn_ref(h, edge_index, edge_weight, batch0, L1_gnn_W1, L1_gnn_b1, L1_gnn_W2, L1_gnn_b2)
    return x

_drawn_inputs = setup_inputs


def setup_inputs(seed=0):
    import zlib

    import numpy as np

    out = dict(_drawn_inputs(seed))
    spreads = {'L1_gnn_b1': (0.0, 0.387), 'L1_gnn_b2': (0.0, 0.1)}
    factors = {'edge_attr_64': 4.411, 'edge_weight': 4.478, 'L0_gnn_b_e': 8.0, 'L0_gnn_b_n': 8.0}
    for name, (base, spread) in spreads.items():
        noise = np.random.default_rng([zlib.crc32(name.encode()), seed]).standard_normal(out[name].shape)
        drawn = base * np.exp(spread * noise) if base else spread * noise
        out[name] = jnp.asarray(drawn.astype(out[name].dtype))
    for name, factor in factors.items():
        out[name] = (out[name] * factor).astype(out[name].dtype)
    return out
```

```python
from contextlib import ExitStack

import concourse.bass as bass
from concourse import mybir

F32 = mybir.dt.float32
I32 = mybir.dt.int32
ALU = mybir.AluOpType
ACT = mybir.ActivationFunctionType
X = mybir.AxisListType.X

P = 128
D = 96
DE = 64
EPS = 1e-5
WIN = 96
EIGHT = 8
GROUP = 7
DX = D + 2


def gnn_program(nc, x, src_tiles, dst_rows, dst_cols, dst_tiles, ew_cols, chunk_base, edge_T,
                W_src, W_dst, W_edge, bias_en, W1, b1, W2, b2, out):
    NODES = out.shape[0]
    NPAD = x.shape[0]
    NB = NPAD // P
    NG = NB // GROUP
    C = src_tiles.shape[0]
    NT = C * EIGHT
    HALF = C // 2
    CE = EIGHT * P
    assert NB % GROUP == 0 and C % 2 == 0

    def turns(eng, n, peeled=1):
        yield from range(peeled)
        with eng.Fori(peeled, n) as i:
            yield i

    def is_at_least(k, least):
        return not isinstance(k, int) or k >= least

    def is_chunk(k):
        return not isinstance(k, int) or 0 <= k < C

    table_src = nc.dram_tensor("table_src", [NPAD, 2 * D], F32).ap()
    table_dst = nc.dram_tensor("table_dst", [NPAD + P, 2 * D], F32).ap()
    tables = [None, nc.dram_tensor("table_1", [NPAD, D], F32).ap(), nc.dram_tensor("table_2", [NPAD, D], F32).ap()]

    with ExitStack() as ctx:
        def sb(name, shape, dt=F32):
            return ctx.enter_context(nc.sbuf_tensor(name, shape, dt))

        def sem(name):
            return ctx.enter_context(nc.semaphore(name))

        x_sb = sb("x_sb", [P, NB, D])
        xh = sb("xh", [P, NB, D])
        sums_T = sb("sums_T", [P, NPAD + P])
        dinv = sb("dinv", [P, NB])
        dst_rel = sb("dst_rel", [P, C, EIGHT])
        dst_i = sb("dst_i", [P, C, EIGHT], I32)
        ew_sb = sb("ew_sb", [P, C, EIGHT])
        stray = sb("stray", [P, C, EIGHT])
        base_b = sb("base_b", [P, C], I32)
        window_node = sb("window_node", [P, C])
        iota_i = sb("iota_i", [P, P], I32)
        iota_f = sb("iota_f", [P, P])
        part_i = sb("part_i", [P, 1], I32)
        part_f = sb("part_f", [P, 1])
        ident_i = sb("ident_i", [P, P], I32)
        ident = sb("ident", [P, P])
        ones = sb("ones", [P, 1])
        w_nodes = sb("w_nodes", [D, 4 * D])
        w_edge = sb("w_edge", [DE, 2 * D])
        bias_sb = sb("bias_sb", [P, 2 * D])
        w_gcn = [None, sb("w1_sb", [D, D]), sb("w2_sb", [D, D])]
        b_gcn = [None, sb("b1_sb", [P, D]), sb("b2_sb", [P, D])]
        strays = sb("strays", [P, 1])
        flag = sb("flag", [1, 1], I32)
        rel = sb("rel", [P, 1])
        msg_one = sb("msg_one", [P, DX])
        hp = sb("hp", [P, NB, D])
        mean = sb("mean", [P, GROUP])
        nmean = sb("nmean", [P, GROUP])
        xc = sb("xc", [P, GROUP, D])
        sq = sb("sq", [P, GROUP, D])
        var = sb("var", [P, GROUP])
        vare = sb("vare", [P, GROUP])
        std = sb("std", [P, GROUP])
        rstd = sb("rstd", [P, GROUP])
        hg = sb("hg", [P, GROUP, D])
        hT = sb("hT", [D, GROUP, P])
        pq = sb("pq", [P, GROUP, 4 * D])
        cnt = sb("cnt", [P, GROUP])
        rcnt = sb("rcnt", [P, GROUP])
        hnew = sb("hnew", [P, GROUP, D])
        deg = sb("deg", [P, GROUP])
        dpos = sb("dpos", [P, GROUP])
        dsafe = sb("dsafe", [P, GROUP])
        dstd = sb("dstd", [P, GROUP])
        drec = sb("drec", [P, GROUP])
        rd = sb("rd", [P, GROUP])
        idx = [sb(f"idx{s}", [P, EIGHT], I32) for s in range(2)]
        rows = [sb(f"rows{s}", [P, EIGHT, 2 * D]) for s in range(2)]
        rows1 = [rows[s][:, :, :].rearrange("p a d -> p (a d)")[:, 0:EIGHT * D].rearrange("p (a d) -> p a d", d=D)
                 for s in range(2)]
        edge_sb = [sb(f"edge{s}", [DE, CE]) for s in range(2)]
        dstw = [sb(f"dstw{s}", [WIN, CE], I32) for s in range(2)]
        dtab = [sb(f"dtab{s}", [WIN, 2 * D]) for s in range(2)]
        hotT = [sb(f"hotT{s}", [WIN, CE]) for s in range(2)]
        hot = [sb(f"hot{s}", [P, EIGHT, WIN]) for s in range(2)]
        hoti = [sb(f"hoti{s}", [P, EIGHT, WIN]) for s in range(2)]
        z = [sb(f"z{s}", [P, EIGHT, 2, D]) for s in range(2)]
        az = [sb(f"az{s}", [P, EIGHT, 2, D]) for s in range(2)]
        msg = [sb(f"msg{s}", [P, EIGHT, DX]) for s in range(2)]
        hot_one = hot[0][:, :, :].rearrange("p j w -> p (j w)")[:, 0:P]
        ps_z = ctx.enter_context(nc.psum_tensor("ps_z", [P, 4, 512], F32))
        ps_w = [ctx.enter_context(nc.psum_tensor(f"ps_w{s}", [P, 512], F32)) for s in range(2)]
        ps_t = ctx.enter_context(nc.psum_tensor("ps_t", [P, 8, P], F32))
        ps_n = ps_z[:, 0:2, :].rearrange("p b (k n) -> p (b k) n", n=P)

        x_in, weights_in, index_in = sem("x_in"), sem("weights_in"), sem("index_in")
        idx_in = [sem(f"idx_in{s}") for s in range(2)]
        edge_in = [sem(f"edge_in{s}") for s in range(2)]
        dtab_in = [sem(f"dtab_in{s}") for s in range(2)]
        dstw_in = [sem(f"dstw_in{s}") for s in range(2)]
        rows_in = [sem(f"rows_in{s}") for s in range(2)]
        table_stored = [sem(f"table{n}_stored") for n in range(3)]
        out_stored = sem("out_stored")
        gathers_let, sums_let = sem("gathers_let"), sem("sums_let")
        ints_made, consts_made, ident_made, zeros_made = sem("ints_made"), sem("consts_made"), sem("ident_made"), sem("zeros_made")
        rel_made, inside_made, stray_made, stray_counted = sem("rel_made"), sem("inside_made"), sem("stray_made"), sem("stray_counted")
        stray_summed, flag_ready = sem("stray_summed"), sem("flag_ready")
        sum_made, nmean_made, xc_made, sq_made = sem("sum_made"), sem("nmean_made"), sem("xc_made"), sem("sq_made")
        var_made, vare_made, std_made, rstd_made = sem("var_made"), sem("vare_made"), sem("std_made"), sem("rstd_made")
        h_made, h_turned, hT_made = sem("h_made"), sem("h_turned"), sem("hT_made")
        node_prod, src_half, dst_half = sem("node_prod"), sem("src_half"), sem("dst_half")
        hotT_made, z_ready, z_added = sem("hotT_made"), sem("z_ready"), sem("z_added")
        absd, expd, logd = sem("absd"), sem("expd"), sem("logd")
        gate_arg, gate_made, plus_made, msg_made = sem("gate_arg"), sem("gate_made"), sem("plus_made"), sem("msg_made")
        equal_made, hot_made, window_done, window_added = sem("equal_made"), sem("hot_made"), sem("window_done"), sem("window_added")
        turned, cnt_made, rcnt_made, hnew_made, x1_made = sem("turned"), sem("cnt_made"), sem("rcnt_made"), sem("hnew_made"), sem("x1_made")
        deg_made, dpos_made, dsafe_made, dstd_made = sem("deg_made"), sem("dpos_made"), sem("dsafe_made"), sem("dstd_made")
        drec_made, dinv_made, rd_made = sem("drec_made"), sem("dinv_made"), sem("rd_made")
        hp_made, hp_turned, sums_init = sem("hp_made"), sem("hp_turned"), sem("sums_init")
        agg_made, scaled_made, biased_made, out_made = sem("agg_made"), sem("scaled_made"), sem("biased_made"), sem("out_made")
        f_next, f_in, f_rows, f_z, f_z1, f_z2 = sem("f_next"), sem("f_in"), sem("f_rows"), sem("f_z"), sem("f_z1"), sem("f_z2")
        f_abs, f_exp, f_log, f_arg, f_plus, f_gate = sem("f_abs"), sem("f_exp"), sem("f_log"), sem("f_arg"), sem("f_plus"), sem("f_gate")
        f_prod, f_msg, f_rel, f_hot, f_sum, f_acc, f_done = (sem("f_prod"), sem("f_msg"), sem("f_rel"), sem("f_hot"), sem("f_sum"),
                                                             sem("f_acc"), sem("f_done"))

        x_v = x.rearrange("(b p) d -> p b d", p=P)
        tsrc_v = table_src.rearrange("(b p) d -> p b d", p=P)
        tdst_v = table_dst[0:NPAD, :].rearrange("(b p) d -> p b d", p=P)
        table_v = [None] + [t.rearrange("(b p) d -> p b d", p=P) for t in tables[1:]]
        N_WEIGHTS, N_INDEX = 8, 3

        def along(a, n):
            return a.unsqueeze(2).to_broadcast([a.shape[0], a.shape[1], n])

        def across(a, k):
            return a.unsqueeze(1).to_broadcast([a.shape[0], k, a.shape[1]])

        def blocks(a, g):
            return a[:, bass.ds(g * GROUP, GROUP), :]

        def columns(a, g):
            return a[:, bass.ds(g * GROUP, GROUP)]

        def sums_of(g):
            return sums_T[0:D, bass.ds(g * (GROUP * P), GROUP * P)].rearrange("d (b n) -> d b n", n=P)

        def any_stray(eng):
            eng.wait_ge(flag_ready, 1)
            return eng.value_load(flag[0:1, 0:1], min_val=0, max_val=NT * P) > 0

        block = ctx.enter_context(nc.Block())

        @block.sync
        def _(sp):
            sp.dma_start(x_sb[:, :, :], x_v).then_inc(x_in, 16)
            for to, of in ((w_nodes[:, 0:2 * D], W_src), (w_nodes[:, 2 * D:], W_dst), (w_edge[:, :], W_edge),
                           (bias_sb[:, :], bias_en.partition_broadcast(P)),
                           (w_gcn[1][:, :], W1), (w_gcn[2][:, :], W2),
                           (b_gcn[1][:, :], b1.partition_broadcast(P)), (b_gcn[2][:, :], b2.partition_broadcast(P))):
                sp.dma_start(to, of).then_inc(weights_in, 16)
            for to, of in ((base_b[:, :], chunk_base.partition_broadcast(P)), (dst_i[:, :, :], dst_cols),
                           (ew_sb[:, :, :], ew_cols)):
                sp.dma_start(to, of).then_inc(index_in, 16)

            def load_idx(k, s):
                sp.dma_start(idx[s][:, :], src_tiles[bass.ds(k, 1), :, :].rearrange("a p j -> (a p) j"))\
                    .then_inc(idx_in[s], 16)

            def load_chunk(k, s):
                sp.dma_start(dstw[s][:, :], dst_rows[bass.ds(k, 1), :].rearrange("a e -> (a e)").partition_broadcast(WIN))\
                    .then_inc(dstw_in[s], 16)
                sp.dma_start(edge_sb[s][:, :], edge_T[:, bass.ds(k * CE, CE)]).then_inc(edge_in[s], 16)
                base = sp.value_load(base_b[0:1, bass.ds(k, 1)], min_val=0, max_val=NPAD - 1)
                sp.dma_start(dtab[s][:, :], table_dst[bass.ds(base, WIN), :]).then_inc(dtab_in[s], 16)

            sp.wait_ge(zeros_made, 1)
            sp.dma_start(table_dst[NPAD:NPAD + P, :], sums_T[:, 0:2 * D]).then_inc(table_stored[0], 16)
            with sp.Fori(0, NG) as g:
                sp.wait_ge(src_half, g * GROUP + GROUP)
                sp.wait_ge(dst_half, g * GROUP + GROUP)
                sp.dma_start(blocks(tsrc_v, g), pq[:, :, 0:2 * D]).then_inc(table_stored[0], 16)
                sp.dma_start(blocks(tdst_v, g), pq[:, :, 2 * D:]).then_inc(table_stored[0], 16)
            sp.wait_ge(table_stored[0], 16 * (2 * NG + 1))
            sp.wait_ge(index_in, 16 * N_INDEX)

            strays_there = any_stray(sp)
            for layer in range(3):
                for i in turns(sp, HALF):
                    for s in range(2):
                        k = i * 2 + s
                        if is_at_least(i, 1):
                            sp.wait_ge(rows_in[s], (i + layer * HALF) * (16 * EIGHT))
                        load_idx(k, s)
                        if layer == 0:
                            if is_at_least(i, 1):
                                sp.wait_ge(z_ready, k * 4 - 4)
                            load_chunk(k, s)
                with sp.If(strays_there):
                    with sp.Fori(0, C) as c:
                        with sp.Fori(0, EIGHT) as j:
                            t = c * EIGHT + j
                            sp.wait_ge(f_next, t + (layer * (NT + 1) + 1))
                            sp.dma_start(idx[0][:, 0:1], src_tiles[bass.ds(c, 1), :, bass.ds(j, 1)]
                                         .rearrange("a p j -> (a p) j"), allow_slow_non_contiguous=True).then_inc(f_in, 16)
                            if layer == 0:
                                sp.dma_start(idx[1][:, 0:1], dst_tiles[bass.ds(c, 1), :, bass.ds(j, 1)]
                                             .rearrange("a p j -> (a p) j"), allow_slow_non_contiguous=True).then_inc(f_in, 16)
                                sp.dma_start(edge_sb[0][:, 0:P], edge_T[:, bass.ds(t * P, P)]).then_inc(f_in, 16)
                    sp.wait_ge(f_done, layer + 1)
                if layer < 2:
                    with sp.Fori(0, NG) as g:
                        sp.wait_ge(hp_made, g + (layer * NG + 1))
                        sp.dma_start(blocks(table_v[layer + 1], g), blocks(hp, g)).then_inc(table_stored[layer + 1], 16)
            full = NODES // P
            for g in range(NG):
                n = min(GROUP, full - g * GROUP)
                sp.wait_ge(out_made, g + 1)
                sp.dma_start(out[g * GROUP * P:(g * GROUP + n) * P, :].rearrange("(b p) d -> p b d", p=P),
                             xh[:, g * GROUP:g * GROUP + n, :]).then_inc(out_stored, 16)
            sp.dma_start(out[full * P:NODES, :], xh[0:NODES - full * P, full, :]).then_inc(out_stored, 16)
            sp.wait_ge(out_stored, 16 * (NG + 1))

        @block.gpsimd
        def _(pool):
            pool.iota(iota_i[:, :], pattern=[[1, P]], base=0, channel_multiplier=0).then_inc(ints_made, 1)
            pool.iota(part_i[:, :], pattern=[[0, 1]], base=0, channel_multiplier=1).then_inc(ints_made, 1)
            pool.iota(ident_i[:, :], pattern=[[1, P]], base=0, channel_multiplier=-1).then_inc(ints_made, 1)

            def gather(to, table, index):
                return pool.indirect_dma_start(out=to, out_offset=None, in_=table,
                                               in_offset=bass.IndirectOffsetOnAxis(ap=index, axis=0))

            strays_there = any_stray(pool)
            for layer in range(3):
                table = table_src if layer == 0 else tables[layer]
                pool.wait_ge(table_stored[layer], 16 * (NG if layer else 2 * NG + 1))
                for i in turns(pool, HALF):
                    for s in range(2):
                        k = i * 2 + s
                        pool.wait_ge(idx_in[s], i * 16 + 16 * (layer * HALF + 1))
                        if is_at_least(i, 1):
                            if layer == 0:
                                pool.wait_ge(z_added, k * 4 - 4)
                            else:
                                pool.wait_ge(window_done, k + (layer * C - 1))
                        pool.sem_inc(gathers_let, 1)
                        to = rows[s] if layer == 0 else rows1[s]
                        for j in range(EIGHT):
                            gather(to[:, j, :], table, idx[s][:, j:j + 1]).then_inc(rows_in[s], 16)
                with pool.If(strays_there):
                    with pool.Fori(0, NT) as t:
                        if layer == 0:
                            pool.wait_ge(f_in, t * 48 + 48)
                            pool.sem_inc(gathers_let, 1)
                            gather(rows[0][:, 0, :], table_src, idx[0][:, 0:1]).then_inc(f_rows, 16)
                            gather(rows[1][:, 0, :], table_dst, idx[1][:, 0:1]).then_inc(f_rows, 16)
                        else:
                            pool.wait_ge(f_in, t * 16 + (48 * NT + 16 * (layer - 1) * NT + 16))
                            pool.sem_inc(gathers_let, 1)
                            gather(rows1[0][:, 0, :], table, idx[0][:, 0:1]).then_inc(f_rows, 16)
                    pool.wait_ge(f_done, layer + 1)

        @block.scalar
        def _(act):
            def square_and_root(g, done):
                act.wait_ge(xc_made, g + (done + 1))
                act.activation(sq[:, :, :], xc[:, :, :], ACT.Square).then_inc(sq_made, 1)
                act.wait_ge(vare_made, g + (done + 1))
                act.activation(std[:, :], vare[:, :], ACT.Sqrt).then_inc(std_made, 1)

            for g in turns(act, NG):
                square_and_root(g, 0)
                act.wait_ge(h_turned, g + 1)
                if is_at_least(g, 1):
                    act.wait_ge(node_prod, g * GROUP)
                act.activation(hT[:, :, :], ps_t[0:D, 0:GROUP, :], ACT.Copy).then_inc(hT_made, 1)
                if is_at_least(g, 1):
                    act.wait_ge(table_stored[0], g * 32 + 16)
                for j in range(GROUP):
                    act.wait_ge(dst_half, g * GROUP + (j + 1))
                    act.activation(pq[:, j, 0:2 * D], ps_z[:, j % 4, 0:2 * D], ACT.Copy).then_inc(src_half, 1)

            def logs(k, s):
                act.wait_ge(z_added, k * 4 + 4)
                if is_at_least(k, 2):
                    act.wait_ge(msg_made, k * 2 - 2)
                act.activation(az[s][:, :, :, :], z[s][:, :, :, :], ACT.Abs).then_inc(absd, 1)
                act.wait_ge(absd, k + 1)
                act.activation(az[s][:, :, :, :], az[s][:, :, :, :], ACT.Exp, scale=-1.0).then_inc(expd, 1)
                act.wait_ge(expd, k + 1)
                act.activation(az[s][:, :, :, :], az[s][:, :, :, :], ACT.Ln, bias=1.0).then_inc(logd, 1)

            def gates(k, s):
                act.wait_ge(gate_arg, k + 1)
                act.activation(az[s][:, :, 0, :], az[s][:, :, 0, :], ACT.Exp).then_inc(gate_made, 1)

            def step(k, s):
                if is_chunk(k - 1):
                    logs(k - 1, 1 - s)
                if is_chunk(k - 2):
                    gates(k - 2, s)

            for i in turns(act, HALF, 2):
                for s in range(2):
                    step(i * 2 + s, s)
            for k in range(C, C + 2):
                step(k, k % 2)

            strays_there = any_stray(act)
            with act.If(strays_there):
                with act.Fori(0, NT) as t:
                    act.wait_ge(f_z2, t + 1)
                    act.activation(az[0][:, 0, :, :], z[0][:, 0, :, :], ACT.Abs).then_inc(f_abs, 1)
                    act.wait_ge(f_abs, t + 1)
                    act.activation(az[0][:, 0, :, :], az[0][:, 0, :, :], ACT.Exp, scale=-1.0).then_inc(f_exp, 1)
                    act.wait_ge(f_exp, t + 1)
                    act.activation(az[0][:, 0, :, :], az[0][:, 0, :, :], ACT.Ln, bias=1.0).then_inc(f_log, 1)
                    act.wait_ge(f_arg, t + 1)
                    act.activation(az[0][:, 0, 0, :], az[0][:, 0, 0, :], ACT.Exp).then_inc(f_gate, 1)
                act.wait_ge(f_done, 1)

            def init_sums(g, done):
                act.wait_ge(hp_turned, g + (done + 1))
                act.activation(sums_of(g), ps_t[0:D, 0:GROUP, :], ACT.Copy).then_inc(sums_init, 1)

            with act.Fori(0, NG) as g:
                square_and_root(g, NG)
                act.wait_ge(dsafe_made, g + 1)
                act.activation(dstd[:, :], dsafe[:, :], ACT.Sqrt).then_inc(dstd_made, 1)
                init_sums(g, 0)
            with act.Fori(0, NG) as g:
                init_sums(g, NG)

        @block.tensor
        def _(pe):
            pe.wait_ge(consts_made, 3)
            pe.wait_ge(ident_made, 1)
            pe.wait_ge(weights_in, 16 * N_WEIGHTS)
            pe.wait_ge(stray_counted, 1)
            pe.matmul(ps_w[0][0:1, 0:1], ones[:, :], strays[:, :], start=True, stop=True).then_inc(stray_summed, 1)

            for g in turns(pe, NG):
                pe.wait_ge(h_made, g + 1)
                if is_at_least(g, 1):
                    pe.wait_ge(hT_made, g)
                for j in range(GROUP):
                    last = pe.transpose(ps_t[0:D, j, :], hg[:, j, :], ident[:, :])
                last.then_inc(h_turned, 1)
                pe.wait_ge(hT_made, g + 1)
                for j in range(GROUP):
                    m = g * GROUP + j
                    if is_at_least(m, 4):
                        pe.wait_ge(src_half, m - 3 + (1 if j < 4 else 0))
                        pe.wait_ge(dst_half, m - 3 + (1 if j < 4 else 0))
                    pe.matmul(ps_z[:, j % 4, 0:4 * D], hT[:, j, :], w_nodes[:, :], start=True, stop=True)\
                        .then_inc(node_prod, 1)

            def products(k, s, i):
                pe.wait_ge(edge_in[s], i * 16 + 16)
                pe.wait_ge(dtab_in[s], i * 16 + 16)
                pe.wait_ge(hotT_made, k + 1)
                for q in range(4):
                    if is_at_least(k, 1):
                        pe.wait_ge(z_added, k * 4 + (q - 3))
                    for j in (2 * q, 2 * q + 1):
                        to = ps_z[:, q, (j % 2) * 2 * D:(j % 2 + 1) * 2 * D]
                        pe.matmul(to, edge_sb[s][:, j * P:(j + 1) * P], w_edge[:, :], start=True, stop=False)
                        last = pe.matmul(to, hotT[s][:, j * P:(j + 1) * P], dtab[s][:, :], start=False, stop=True)
                    last.then_inc(z_ready, 1)

            def window(K, s, rows_of, width):
                pe.wait_ge(hot_made, K + 1)
                if is_at_least(K, 2):
                    pe.wait_ge(window_added, K - 1)
                for j in range(EIGHT):
                    last = pe.matmul(ps_w[s][0:width, 0:WIN], rows_of[:, j, :], hot[s][:, j, :],
                                     start=(j == 0), stop=(j == EIGHT - 1))
                last.then_inc(window_done, 1)

            def first_layer_step(k, s, i):
                if is_chunk(k - 3):
                    pe.wait_ge(msg_made, k * 2 - 4)
                    window(k - 3, 1 - s, msg[1 - s], DX)
                if is_chunk(k):
                    products(k, s, i)

            def stray_windows(layer, t):
                with pe.Fori(0, NB) as w:
                    n = t * NB + w
                    pe.wait_ge(f_hot, n + (layer * NT * NB + 1))
                    pe.matmul(ps_w[0][0:DX, 0:P], msg_one[:, :], hot_one, start=True, stop=True).then_inc(f_sum, 1)

            strays_there = any_stray(pe)
            for i in turns(pe, HALF, 2):
                for s in range(2):
                    first_layer_step(i * 2 + s, s, i)
            for k in range(C, C + 3):
                first_layer_step(k, k % 2, None)
            with pe.If(strays_there):
                with pe.Fori(0, NT) as t:
                    pe.wait_ge(f_in, t * 48 + 48)
                    pe.matmul(ps_z[:, 0, 0:2 * D], edge_sb[0][:, 0:P], w_edge[:, :], start=True, stop=True)\
                        .then_inc(f_z, 1)
                    stray_windows(0, t)
                pe.wait_ge(f_done, 1)

            def turn_rows(g, done):
                pe.wait_ge(hp_made, g + (done + 1))
                if is_at_least(g, 1):
                    pe.wait_ge(sums_init, g + done)
                for j in range(GROUP):
                    last = pe.transpose(ps_t[0:D, j, :], hp[:, bass.ds(g * GROUP + j, 1), :].rearrange("p a d -> p (a d)"),
                                        ident[:, :])
                last.then_inc(hp_turned, 1)

            def sums_block(g, j, rows_n):
                return sums_T[0:rows_n, bass.ds(g * (GROUP * P) + j * P, P)]

            pe.wait_ge(window_added, C)
            for g in range(NG):
                if is_at_least(g, 1):
                    pe.wait_ge(hnew_made, g)
                    pe.wait_ge(deg_made, g)
                for j in range(GROUP):
                    last = pe.transpose(ps_n[:, j, 0:DX], sums_block(g, j, DX), ident[0:DX, 0:DX])
                last.then_inc(turned, 1)
                turn_rows(g, 0)

            for layer in (1, 2):
                for i in turns(pe, HALF):
                    for s in range(2):
                        pe.wait_ge(rows_in[s], i * (16 * EIGHT) + (layer * HALF + 1) * 16 * EIGHT)
                        window(i * 2 + (layer * C + s), s, rows1[s], D)
                with pe.If(strays_there):
                    with pe.Fori(0, NT) as t:
                        stray_windows(layer, t)
                    pe.wait_ge(f_done, layer + 1)
                pe.wait_ge(window_added, (layer + 1) * C)
                for g in range(NG):
                    if is_at_least(g, 1):
                        pe.wait_ge(scaled_made, g + (layer - 1) * NG)
                    for j in range(GROUP):
                        last = pe.matmul(ps_n[:, j, 0:D], sums_block(g, j, D), w_gcn[layer][:, :], start=True, stop=True)
                    last.then_inc(agg_made, 1)
                    if layer == 1:
                        turn_rows(g, NG)

        @block.vector
        def _(dve):
            TT, TS = dve.tensor_tensor, dve.tensor_scalar
            dve.memset(sums_T[:, :], 0.0).then_inc(zeros_made, 1)
            dve.memset(ones[:, :], 1.0).then_inc(consts_made, 1)
            for s in range(2):
                dve.memset(msg[s][:, :, D:D + 1], 1.0)
            dve.memset(msg_one[:, :], 0.0)
            dve.wait_ge(ints_made, 3)
            dve.tensor_copy(iota_f[:, :], iota_i[:, :]).then_inc(consts_made, 1)
            dve.tensor_copy(part_f[:, :], part_i[:, :]).then_inc(consts_made, 1)
            TS(ident[:, :], ident_i[:, :], 0.0, None, ALU.is_equal).then_inc(ident_made, 1)
            dve.wait_ge(consts_made, 3)
            dve.wait_ge(index_in, 16 * N_INDEX)
            TS(window_node[:, :], base_b[:, :], part_f[:, :], None, ALU.add)
            TT(dst_rel[:, :, :], dst_i[:, :, :], along(base_b[:, :], EIGHT), ALU.subtract).then_inc(rel_made, 1)
            dve.wait_ge(rel_made, 1)
            TS(stray[:, :, :], dst_rel[:, :, :], float(WIN), None, ALU.is_ge).then_inc(inside_made, 1)
            dve.wait_ge(inside_made, 1)
            dve.scalar_tensor_tensor(out=stray[:, :, :], in0=dst_rel[:, :, :], scalar=0.0, in1=stray[:, :, :],
                                     op0=ALU.is_lt, op1=ALU.add).then_inc(stray_made, 1)
            dve.wait_ge(stray_made, 1)
            dve.reduce_sum(strays[:, :], stray[:, :, :].rearrange("p c j -> p (c j)"), X).then_inc(stray_counted, 1)
            dve.wait_ge(stray_summed, 1)
            dve.tensor_copy(flag[:, :], ps_w[0][0:1, 0:1]).then_inc(flag_ready, 1)

            def layernorm(g, done):
                n = g + (done + 1)
                dve.sem_inc(sums_let, 1)
                dve.reduce_sum(mean[:, :], blocks(x_sb, g), X).then_inc(sum_made, 1)
                dve.wait_ge(sum_made, n)
                TS(nmean[:, :], mean[:, :], -1.0 / D, None, ALU.mult).then_inc(nmean_made, 1)
                dve.wait_ge(nmean_made, n)
                TT(xc[:, :, :], blocks(x_sb, g), along(nmean[:, :], D), ALU.add).then_inc(xc_made, 1)
                dve.wait_ge(sq_made, n)
                dve.reduce_sum(var[:, :], sq[:, :, :], X).then_inc(var_made, 1)
                dve.wait_ge(var_made, n)
                TS(vare[:, :], var[:, :], 1.0 / D, EPS, ALU.mult, ALU.add).then_inc(vare_made, 1)
                dve.wait_ge(std_made, n)
                dve.reciprocal(rstd[:, :], std[:, :]).then_inc(rstd_made, 1)
                dve.wait_ge(rstd_made, n)

            def relu_times(out, a, scale):
                return dve.scalar_tensor_tensor(out=out, in0=a, scalar=0.0, in1=along(scale, D), op0=ALU.max, op1=ALU.mult)

            dve.wait_ge(x_in, 16)
            dve.wait_ge(weights_in, 16 * N_WEIGHTS)
            for g in turns(dve, NG):
                layernorm(g, 0)
                if is_at_least(g, 1):
                    dve.wait_ge(h_turned, g)
                relu_times(hg[:, :, :], xc[:, :, :], rstd[:, :]).then_inc(h_made, 1)
                dve.wait_ge(h_made, g + 1)
                TT(blocks(xh, g), blocks(x_sb, g), hg[:, :, :], ALU.add)
                if is_at_least(g, 1):
                    dve.wait_ge(table_stored[0], g * 32 + 16)
                for j in range(GROUP):
                    dve.wait_ge(node_prod, g * GROUP + (j + 1))
                    TT(pq[:, j, 2 * D:], ps_z[:, j % 4, 2 * D:4 * D], bias_sb[:, :], ALU.add).then_inc(dst_half, 1)

            def targets_hot(k, s, i):
                dve.wait_ge(dstw_in[s], i * 16 + 16)
                TS(hotT[s][:, :], dstw[s][:, :], window_node[0:WIN, bass.ds(k, 1)], None, ALU.is_equal)\
                    .then_inc(hotT_made, 1)

            def add_sources(k, s, i):
                dve.wait_ge(rows_in[s], i * (16 * EIGHT) + 16 * EIGHT)
                if is_at_least(k, 2):
                    dve.wait_ge(plus_made, k - 1)
                for q in range(4):
                    dve.wait_ge(z_ready, k * 4 + (q + 1))
                    TT(z[s][:, 2 * q:2 * q + 2, :, :].rearrange("p a b d -> p (a b d)"), ps_z[:, q, 0:4 * D],
                       rows[s][:, 2 * q:2 * q + 2, :].rearrange("p a d -> p (a d)"), ALU.add).then_inc(z_added, 1)

            def sum_args(k, s):
                dve.wait_ge(logd, k + 1)
                dve.scalar_tensor_tensor(out=az[s][:, :, 0, :], in0=z[s][:, :, 0, :], scalar=0.0, in1=az[s][:, :, 0, :],
                                         op0=ALU.min, op1=ALU.subtract).then_inc(gate_arg, 1)
                dve.scalar_tensor_tensor(out=az[s][:, :, 1, :], in0=z[s][:, :, 1, :], scalar=0.0, in1=az[s][:, :, 1, :],
                                         op0=ALU.max, op1=ALU.add).then_inc(plus_made, 1)

            def messages(k, s):
                dve.wait_ge(gate_made, k + 1)
                dve.wait_ge(plus_made, k + 1)
                TT(msg[s][:, :, 0:D], az[s][:, :, 0, :], az[s][:, :, 1, :], ALU.mult).then_inc(msg_made, 1)
                dve.tensor_copy(msg[s][:, :, D + 1:DX].rearrange("p j a -> p (j a)"),
                                ew_sb[:, bass.ds(k, 1), :].rearrange("p a j -> p (a j)")).then_inc(msg_made, 1)

            def targets(k, s, K, weighted):
                rel_k = dst_rel[:, bass.ds(k, 1), :].rearrange("p a j -> p (a j)")
                to = hoti[s] if weighted else hot[s]
                if weighted:
                    dve.wait_ge(hot_made, K - 1)
                made = TT(to[:, :, :], across(iota_f[:, 0:WIN], EIGHT), along(rel_k, WIN), ALU.is_equal)
                if not weighted:
                    made.then_inc(hot_made, 1)
                    return
                made.then_inc(equal_made, 1)
                dve.wait_ge(equal_made, K - C + 1)
                TT(hot[s][:, :, :], hoti[s][:, :, :], along(ew_sb[:, bass.ds(k, 1), :].rearrange("p a j -> p (a j)"), WIN),
                   ALU.mult).then_inc(hot_made, 1)

            def add_window(k, s, K, width):
                base = dve.value_load(base_b[0:1, bass.ds(k, 1)], min_val=0, max_val=NPAD - 1)
                at = sums_T[0:width, bass.ds(base, WIN)]
                dve.wait_ge(window_done, K + 1)
                if is_at_least(K, 1):
                    dve.wait_ge(window_added, K)
                TT(at, at, ps_w[s][0:width, 0:WIN], ALU.add).then_inc(window_added, 1)

            def first_layer_step(k, s, i):
                if is_chunk(k):
                    targets_hot(k, s, i)
                if is_chunk(k - 1):
                    add_sources(k - 1, 1 - s, i if s else i - 1)
                if is_chunk(k - 3):
                    messages(k - 3, 1 - s)
                if is_chunk(k - 2):
                    sum_args(k - 2, s)
                if is_chunk(k - 3):
                    add_window(k - 3, 1 - s, k - 3, DX)
                if is_chunk(k - 1):
                    targets(k - 1, 1 - s, k - 1, False)

            def strays_of(layer):
                dve.drain().then_inc(f_next, 1)
                with dve.Fori(0, C) as c:
                    with dve.Fori(0, EIGHT) as j:
                        t = c * EIGHT + j
                        T = t + layer * NT
                        stray_t = stray[:, bass.ds(c, 1), bass.ds(j, 1)].rearrange("p a b -> p (a b)")
                        ew_t = ew_sb[:, bass.ds(c, 1), bass.ds(j, 1)].rearrange("p a b -> p (a b)")
                        dst_t = dst_i[:, bass.ds(c, 1), bass.ds(j, 1)].rearrange("p a b -> p (a b)")
                        if layer == 0:
                            zt, at = z[0][:, 0, :, :], az[0][:, 0, :, :]
                            flat = zt.rearrange("p b d -> p (b d)")
                            dve.wait_ge(f_rows, t * 32 + 32)
                            dve.wait_ge(f_z, t + 1)
                            TT(flat, ps_z[:, 0, 0:2 * D], rows[0][:, 0, :], ALU.add).then_inc(f_z1, 1)
                            dve.wait_ge(f_z1, t + 1)
                            TT(flat, flat, rows[1][:, 0, :], ALU.add).then_inc(f_z2, 1)
                            dve.wait_ge(f_z2, t + 1)
                            dve.wait_ge(f_log, t + 1)
                            dve.scalar_tensor_tensor(out=at[:, 0, :], in0=zt[:, 0, :], scalar=0.0, in1=at[:, 0, :],
                                                     op0=ALU.min, op1=ALU.subtract).then_inc(f_arg, 1)
                            dve.scalar_tensor_tensor(out=at[:, 1, :], in0=zt[:, 1, :], scalar=0.0, in1=at[:, 1, :],
                                                     op0=ALU.max, op1=ALU.add).then_inc(f_plus, 1)
                            dve.tensor_copy(msg[0][:, 0, D + 1:DX], ew_t).then_inc(f_prod, 1)
                            dve.wait_ge(f_plus, t + 1)
                            dve.wait_ge(f_gate, t + 1)
                            TT(msg[0][:, 0, 0:D], at[:, 0, :], at[:, 1, :], ALU.mult).then_inc(f_prod, 1)
                            dve.wait_ge(f_prod, t * 2 + 2)
                            TS(msg_one[:, :], msg[0][:, 0, :], stray_t, None, ALU.mult).then_inc(f_msg, 1)
                        else:
                            dve.wait_ge(f_rows, t * 16 + (32 * NT + 16 * (layer - 1) * NT + 16))
                            TS(msg_one[:, 0:D], rows1[0][:, 0, :], stray_t, ew_t, ALU.mult, ALU.mult).then_inc(f_msg, 1)
                        dve.tensor_copy(rel[:, :], dst_t).then_inc(f_rel, 1)
                        with dve.Fori(0, NB) as w:
                            n = T * NB + w
                            dve.wait_ge(f_msg, T + 1)
                            dve.wait_ge(f_rel, n + T + 1)
                            TS(hot_one, iota_f[:, :], rel[:, :], None, ALU.is_equal).then_inc(f_hot, 1)
                            dve.wait_ge(f_hot, n + 1)
                            TS(rel[:, :], rel[:, :], float(-P), None, ALU.add).then_inc(f_rel, 1)
                            at_w = sums_T[0:DX, bass.ds(w * P, P)]
                            dve.wait_ge(f_sum, n + 1)
                            TT(at_w, at_w, ps_w[0][0:DX, 0:P], ALU.add).then_inc(f_acc, 1)
                            dve.wait_ge(f_acc, n + 1)
                        dve.drain().then_inc(f_next, 1)
                dve.drain().then_inc(f_done, 1)

            strays_there = any_stray(dve)
            for i in turns(dve, HALF, 2):
                for s in range(2):
                    first_layer_step(i * 2 + s, s, i)
            for k in range(C, C + 3):
                first_layer_step(k, k % 2, k // 2)
            dve.wait_ge(window_added, C)
            with dve.If(strays_there):
                strays_of(0)

            with dve.Fori(0, NG) as g:
                n = g + 1
                dve.wait_ge(turned, n)
                TS(cnt[:, :], ps_n[:, 0:GROUP, D], 1.0, None, ALU.max).then_inc(cnt_made, 1)
                TS(deg[:, :], ps_n[:, 0:GROUP, D + 1], 1.0, None, ALU.add).then_inc(deg_made, 1)
                dve.wait_ge(cnt_made, n)
                dve.reciprocal(rcnt[:, :], cnt[:, :]).then_inc(rcnt_made, 1)
                dve.wait_ge(rcnt_made, n)
                TT(hnew[:, :, :], ps_n[:, 0:GROUP, 0:D], along(rcnt[:, :], D), ALU.mult).then_inc(hnew_made, 1)
                dve.wait_ge(hnew_made, n)
                TT(blocks(x_sb, g), hnew[:, :, :], blocks(xh, g), ALU.add).then_inc(x1_made, 1)
                dve.wait_ge(x1_made, n)
                layernorm(g, NG)
                dve.wait_ge(deg_made, n)
                TS(dpos[:, :], deg[:, :], 0.0, None, ALU.is_gt).then_inc(dpos_made, 1)
                TS(dsafe[:, :], deg[:, :], 1e-30, None, ALU.max).then_inc(dsafe_made, 1)
                dve.wait_ge(dstd_made, n)
                dve.reciprocal(drec[:, :], dstd[:, :]).then_inc(drec_made, 1)
                dve.wait_ge(drec_made, n)
                dve.wait_ge(dpos_made, n)
                TT(columns(dinv, g), drec[:, :], dpos[:, :], ALU.mult).then_inc(dinv_made, 1)
                dve.wait_ge(dinv_made, n)
                TT(rd[:, :], rstd[:, :], columns(dinv, g), ALU.mult).then_inc(rd_made, 1)
                dve.wait_ge(rd_made, n)
                relu_times(blocks(hp, g), xc[:, :, :], rd[:, :]).then_inc(hp_made, 1)

            for layer in (1, 2):
                dve.wait_ge(sums_init, layer * NG)
                for i in turns(dve, HALF):
                    for s in range(2):
                        k = i * 2 + s
                        targets(k, s, k + layer * C, True)
                        if is_chunk(k - 1):
                            add_window(k - 1, 1 - s, k + (layer * C - 1), D)
                add_window(C - 1, 1, (layer + 1) * C - 1, D)
                dve.wait_ge(window_added, (layer + 1) * C)
                with dve.If(strays_there):
                    strays_of(layer)
                if layer == 1:
                    dve.wait_ge(table_stored[1], 16 * NG)
                with dve.Fori(0, NG) as g:
                    n = g + ((layer - 1) * NG + 1)
                    dve.wait_ge(agg_made, n)
                    TT(xc[:, :, :], ps_n[:, 0:GROUP, 0:D], along(columns(dinv, g), D), ALU.mult).then_inc(scaled_made, 1)
                    dve.wait_ge(scaled_made, n)
                    TT(sq[:, :, :], xc[:, :, :], across(b_gcn[layer][:, :], GROUP), ALU.add).then_inc(biased_made, 1)
                    dve.wait_ge(biased_made, n)
                    if layer == 1:
                        relu_times(blocks(hp, g), sq[:, :, :], columns(dinv, g)).then_inc(hp_made, 1)
                    else:
                        dve.scalar_tensor_tensor(out=blocks(xh, g), in0=sq[:, :, :], scalar=0.0, in1=blocks(x_sb, g),
                                                 op0=ALU.max, op1=ALU.add).then_inc(out_made, 1)


def kernel(x, src, dst, edge_attr_64, edge_weight, L0_gnn_W_e, L0_gnn_b_e, L0_gnn_W_n, L0_gnn_b_n,
           L1_gnn_W1, L1_gnn_b1, L1_gnn_W2, L1_gnn_b2):
    import numpy as np
    import concourse.bacc as bacc
    from concourse.bass_utils import run_bass_kernel_spmd as run

    nodes, edges = x.shape[0], src.shape[0]
    node_pad = -nodes % (P * GROUP)
    tile_pad = -edges % (2 * P * EIGHT)
    chunks = (edges + tile_pad) // (P * EIGHT)
    x = np.pad(np.asarray(x), ((0, node_pad), (0, 0)))
    src = np.pad(np.asarray(src), (0, tile_pad)).reshape(chunks, EIGHT, P)
    dst = np.pad(np.asarray(dst), (0, tile_pad), constant_values=nodes).reshape(chunks, EIGHT, P)
    ew = np.pad(np.asarray(edge_weight), (0, tile_pad)).reshape(chunks, EIGHT, P)
    edge_T = np.pad(np.asarray(edge_attr_64), ((0, tile_pad), (0, 0))).T
    W_e, W_n = np.asarray(L0_gnn_W_e), np.asarray(L0_gnn_W_n)
    both = np.concatenate([W_e, W_n], axis=1)
    arrays = {
        "x": x, "src_tiles": src.transpose(0, 2, 1), 
        "dst_rows": dst.reshape(chunks, EIGHT * P), "dst_cols": dst.transpose(2, 0, 1), "dst_tiles": dst.transpose(0, 2, 1),
        "ew_cols": ew.transpose(2, 0, 1), "chunk_base": dst[:, 0, 0], "edge_T": edge_T,
        "W_src": both[0:D], "W_dst": both[D:2 * D], "W_edge": both[2 * D:],
        "bias_en": np.concatenate([np.asarray(L0_gnn_b_e), np.asarray(L0_gnn_b_n)]),
        "W1": np.asarray(L1_gnn_W1), "b1": np.asarray(L1_gnn_b1), "W2": np.asarray(L1_gnn_W2), "b2": np.asarray(L1_gnn_b2),
    }
    nc = bacc.Bacc("TRN2", target_bir_lowering=False, num_devices=1)
    args, feeds = {}, {}
    for name, a in arrays.items():
        feeds[f"in_{name}"] = a = np.ascontiguousarray(a)
        args[name] = nc.dram_tensor(f"in_{name}", a.shape, mybir.dt.from_np(a.dtype), kind="ExternalInput").ap()
    args["out"] = nc.dram_tensor("out_0", (nodes, D), F32, kind="ExternalOutput").ap()
    gnn_program(nc, **args)
    return run(nc, [feeds], core_ids=[0]).results[0]["out_0"]
```

```python
from contextlib import ExitStack

import concourse.bass as bass
from concourse import mybir

F32 = mybir.dt.float32
I32 = mybir.dt.int32
ALU = mybir.AluOpType
ACT = mybir.ActivationFunctionType
X = mybir.AxisListType.X

P = 128
D = 96
DE = 64
EPS = 1e-5
WIN = 96
EIGHT = 8
GROUP = 7
LEAD = 3
DX = D + 2


def gnn_program(nc, x, src_tiles, dst_rows, dst_cols, dst_tiles, ew_cols, chunk_base, edge_T,
                W_nodes, W_edge, W1, b1, W2, b2, out):
    NODES = out.shape[0]
    NPAD = x.shape[0]
    NB = NPAD // P
    NG = NB // GROUP
    C = src_tiles.shape[0]
    NT = C * EIGHT
    HALF = C // 2
    PAIRS = HALF // NG
    CE = EIGHT * P
    GP = GROUP * P
    assert NB % GROUP == 0 and C % 2 == 0 and HALF % NG == 0 and PAIRS >= LEAD + 3 and NG >= 2

    def schedule(eng):
        for i in range(2):
            yield "pair", i
        with eng.Fori(2, PAIRS) as i:
            yield "pair", i
        with eng.Fori(1, NG) as g:
            with eng.Fori(0, LEAD) as i:
                yield "pair", g * PAIRS + i
            yield "a", g - 1
            yield "pair", g * PAIRS + LEAD
            yield "b", g - 1
            yield "pair", g * PAIRS + (LEAD + 1)
            yield "c", g - 1
            with eng.Fori(LEAD + 2, PAIRS) as i:
                yield "pair", g * PAIRS + i
            yield "d", g - 1

    def is_at_least(k, least):
        return not isinstance(k, int) or k >= least

    def is_chunk(k):
        return not isinstance(k, int) or 0 <= k < C

    table_src = nc.dram_tensor("table_src", [NPAD, 2 * D], F32).ap()
    table_dst = nc.dram_tensor("table_dst", [NPAD + P, 2 * D], F32).ap()
    tables = [None, nc.dram_tensor("table_1", [NPAD, D], F32).ap(), nc.dram_tensor("table_2", [NPAD, D], F32).ap()]

    with ExitStack() as ctx:
        def sb(name, shape, dt=F32):
            return ctx.enter_context(nc.sbuf_tensor(name, shape, dt))

        def sem(name):
            return ctx.enter_context(nc.semaphore(name))

        x_sb = sb("x_sb", [P, NB, D])
        xh = sb("xh", [P, NB, D])
        sums = [sb(f"sums{n}", [P, NPAD + P]) for n in range(2)]
        dinv = sb("dinv", [P, NB])
        dst_rel = sb("dst_rel", [P, C, EIGHT])
        dst_i = sb("dst_i", [P, C, EIGHT], I32)
        ew_sb = sb("ew_sb", [P, C, EIGHT])
        stray = sb("stray", [P, C, EIGHT])
        base_b = sb("base_b", [P, C], I32)
        window_node = sb("window_node", [P, C])
        iota_i = sb("iota_i", [P, P], I32)
        iota_f = sb("iota_f", [P, P])
        part_i = sb("part_i", [P, 1], I32)
        part_f = sb("part_f", [P, 1])
        ident_i = sb("ident_i", [P, P], I32)
        ident = sb("ident", [P, P])
        ones = sb("ones", [P, 1])
        w_nodes = sb("w_nodes", [D + 1, 4 * D])
        w_edge = sb("w_edge", [DE, 2 * D])
        w_gcn = [None, sb("w1_sb", [D, D]), sb("w2_sb", [D, D])]
        b_gcn = [None, sb("b1_sb", [P, D]), sb("b2_sb", [P, D])]
        first_node = sb("first_node", [P, C + LEAD], I32)
        late = sb("late", [P, C, EIGHT])
        strays = sb("strays", [P, 2])
        flag = sb("flag", [1, 1], I32)
        rel = sb("rel", [P, 1])
        msg_one = sb("msg_one", [P, DX])
        total = sb("total", [P, GROUP])
        nmean = sb("nmean", [P, GROUP])
        xc = sb("xc", [P, GROUP, D])
        sq = sb("sq", [P, GROUP, D])
        var = sb("var", [P, GROUP])
        root_in = sb("root_in", [P, 2 * GROUP])
        root = sb("root", [P, 2 * GROUP])
        rroot = sb("rroot", [P, 2 * GROUP])
        staged_T = sb("staged_T", [P, GP])
        new_rows = sb("new_rows", [P, GROUP, D])
        cnt = sb("cnt", [P, GROUP])
        rcnt = sb("rcnt", [P, GROUP])
        dpos = sb("dpos", [P, GROUP])
        rd = sb("rd", [P, GROUP])
        idx = [sb(f"idx{s}", [P, EIGHT], I32) for s in range(2)]
        rows = [sb(f"rows{s}", [P, EIGHT, 2 * D]) for s in range(2)]
        rows1 = [rows[s][:, :, :].rearrange("p a d -> p (a d)")[:, 0:EIGHT * D].rearrange("p (a d) -> p a d", d=D)
                 for s in range(2)]
        edge_sb = [sb(f"edge{s}", [DE, CE]) for s in range(2)]
        dstw = [sb(f"dstw{s}", [WIN, CE], I32) for s in range(2)]
        dtab = [sb(f"dtab{s}", [WIN, 2 * D]) for s in range(2)]
        hot_mem = [sb(f"hotT{s}", [P, CE]) for s in range(2)]
        hotT = [m[0:WIN, :] for m in hot_mem]
        hot = [sb(f"hot{s}", [P, EIGHT, WIN]) for s in range(2)]
        hoti = [m[:, 0:EIGHT * WIN].rearrange("p (j w) -> p j w", w=WIN) for m in hot_mem]
        ZW = EIGHT * 2 * D
        work = sb("work", [P, 4 * ZW])
        z, az = ([work[:, (2 * n + s) * ZW:(2 * n + s + 1) * ZW].rearrange("p (j h d) -> p j h d", h=2, d=D)
                  for s in range(2)] for n in range(2))
        PQ = GROUP * 4 * D
        pq = [work[:, s * PQ:(s + 1) * PQ].rearrange("p (b n) -> p b n", n=4 * D) for s in range(2)]
        hT = [rows[s][0:D + 1, :, :].rearrange("p a d -> p (a d)")[:, 0:GP].rearrange("p (b n) -> p b n", n=P)
              for s in range(2)]
        xc_all = sums[1][:, 0:NB * D].rearrange("p (b d) -> p b d", d=D)
        msg = [sb(f"msg{s}", [P, EIGHT, DX]) for s in range(2)]
        hot_one = hot[0][:, :, :].rearrange("p j w -> p (j w)")[:, 0:P]
        ps_z = ctx.enter_context(nc.psum_tensor("ps_z", [P, 4, 512], F32))
        ps_w = [ctx.enter_context(nc.psum_tensor(f"ps_w{s}", [P, 512], F32)) for s in range(2)]
        ps_t = ctx.enter_context(nc.psum_tensor("ps_t", [P, 8, P], F32))

        x_in = [sem(f"x_in{g}") for g in range(NG)]
        weights_in, index_in = sem("weights_in"), sem("index_in")
        idx_in = [sem(f"idx_in{s}") for s in range(2)]
        edge_in = [sem(f"edge_in{s}") for s in range(2)]
        dtab_in = [sem(f"dtab_in{s}") for s in range(2)]
        dstw_in = [sem(f"dstw_in{s}") for s in range(2)]
        rows_in = [sem(f"rows_in{s}") for s in range(2)]
        tail_stored = sem("tail_stored")
        pq_stored = [sem(f"pq{s}_stored") for s in range(2)]
        gathers_let, sums_let = sem("gathers_let"), sem("sums_let")
        ints_made, consts_made, ident_made, zeros_made = sem("ints_made"), sem("consts_made"), sem("ident_made"), sem("zeros_made")
        rel_made, inside_made, stray_made, stray_counted = sem("rel_made"), sem("inside_made"), sem("stray_made"), sem("stray_counted")
        first_node_made = sem("first_node_made")
        late_made, stray_summed, flag_ready = sem("late_made"), sem("stray_summed"), sem("flag_ready")
        p_total, p_nmean, p_xc, p_sq, p_var, p_root_in, p_root, p_rroot = (
            sem(f"p_{n}") for n in "total nmean xc sq var root_in root rroot".split())
        h_made, xh_made, h_turned, hT_made = sem("h_made"), sem("xh_made"), sem("h_turned"), sem("hT_made")
        node_prod, copied_act, copied_dve = sem("node_prod"), sem("copied_act"), sem("copied_dve")
        hotT_made, z_ready, z_added = sem("hotT_made"), sem("z_ready"), sem("z_added")
        absd, expd, logd = sem("absd"), sem("expd"), sem("logd")
        gate_arg, gate_made, plus_made, msg_made = sem("gate_arg"), sem("gate_made"), sem("plus_made"), sem("msg_made")
        equal_made, hot_made, window_done, window_added = sem("equal_made"), sem("hot_made"), sem("window_done"), sem("window_added")
        class Taking:
            def __init__(self, name, per_layer):
                self.per_layer = per_layer
                (self.staged, self.turned, self.rows_turned, self.t_free, self.rows_free, self.rows_made, self.cnt, self.rcnt,
                 self.dpos, self.hnew, self.x1, self.total, self.nmean, self.xc, self.sq, self.var, self.root_in, self.root,
                 self.rroot, self.dinv, self.rd, self.scaled, self.biased) = (sem(f"{name}_{what}") for what in (
                     "staged turned rows_turned t_free rows_free rows_made cnt rcnt dpos hnew x1 total nmean xc sq var "
                     "root_in root rroot dinv rd scaled biased").split())
                self.stored = [sem(f"{name}_stored{n}") for n in range(1, 4)]

            def count(self, layer, g):
                return g + (layer * self.per_layer + 1)

        first_take, retake = Taking("take", NG), Taking("retake", NG - 1)
        retaken = sem("retaken")
        f_next, f_in, f_rows, f_z, f_z1, f_z2 = sem("f_next"), sem("f_in"), sem("f_rows"), sem("f_z"), sem("f_z1"), sem("f_z2")
        f_abs, f_exp, f_log, f_arg, f_plus, f_gate = sem("f_abs"), sem("f_exp"), sem("f_log"), sem("f_arg"), sem("f_plus"), sem("f_gate")
        f_prod, f_msg, f_rel, f_hot, f_sum, f_acc = (sem("f_prod"), sem("f_msg"), sem("f_rel"), sem("f_hot"), sem("f_sum"),
                                                     sem("f_acc"))

        x_v = x.rearrange("(b p) d -> p b d", p=P)
        tsrc_v = table_src.rearrange("(b p) d -> p b d", p=P)
        tdst_v = table_dst[0:NPAD, :].rearrange("(b p) d -> p b d", p=P)
        table_v = [t.rearrange("(b p) d -> p b d", p=P) for t in tables[1:]]
        N_WEIGHTS, N_INDEX = 6, 3

        def along(a, n):
            return a.unsqueeze(2).to_broadcast([a.shape[0], a.shape[1], n])

        def across(a, k):
            return a.unsqueeze(1).to_broadcast([a.shape[0], k, a.shape[1]])

        def blocks(a, g):
            if isinstance(g, int):
                return a[:, g * GROUP:(g + 1) * GROUP, :]
            return a[:, bass.ds(g * GROUP, GROUP), :]

        def columns(a, g):
            return a[:, bass.ds(g * GROUP, GROUP)]

        def sums_of(layer, g, n):
            return sums[layer % 2][0:n, bass.ds(g * GP, GP)]

        def is_last(g):
            return isinstance(g, int) and g == NG - 1

        def first_tables_stored(eng):
            eng.wait_ge(tail_stored, 16)
            for s in range(2):
                eng.wait_ge(pq_stored[s], 32 * len(range(s, NG, 2)))

        def any_stray(eng):
            eng.wait_ge(flag_ready, 1)
            return eng.value_load(flag[0:1, 0:1], min_val=0, max_val=NT * P) > 0

        block = ctx.enter_context(nc.Block())

        @block.sync
        def _(sp):
            sp.dma_start(blocks(x_sb, 0), blocks(x_v, 0)).then_inc(x_in[0], 16)
            sp.dma_start(w_nodes[:, :], W_nodes).then_inc(weights_in, 16)
            for g in range(1, NG):
                sp.dma_start(blocks(x_sb, g), blocks(x_v, g)).then_inc(x_in[g], 16)
            for to, of in ((w_edge[:, :], W_edge), (w_gcn[1][:, :], W1), (w_gcn[2][:, :], W2),
                           (b_gcn[1][:, :], b1.partition_broadcast(P)), (b_gcn[2][:, :], b2.partition_broadcast(P))):
                sp.dma_start(to, of).then_inc(weights_in, 16)
            for to, of in ((base_b[:, :], chunk_base.partition_broadcast(P)), (dst_i[:, :, :], dst_cols),
                           (ew_sb[:, :, :], ew_cols)):
                sp.dma_start(to, of).then_inc(index_in, 16)

            def load_idx(k, s):
                sp.dma_start(idx[s][:, :], src_tiles[bass.ds(k, 1), :, :].rearrange("a p j -> (a p) j"))\
                    .then_inc(idx_in[s], 16)

            def load_chunk(k, s):
                sp.dma_start(dstw[s][:, :], dst_rows[bass.ds(k, 1), :].rearrange("a e -> (a e)").partition_broadcast(WIN))\
                    .then_inc(dstw_in[s], 16)
                sp.dma_start(edge_sb[s][:, :], edge_T[:, bass.ds(k * CE, CE)]).then_inc(edge_in[s], 16)
                if not is_at_least(k, 2):
                    first_tables_stored(sp)
                base = sp.value_load(base_b[0:1, bass.ds(k, 1)], min_val=0, max_val=NPAD - 1)
                sp.dma_start(dtab[s][:, :], table_dst[bass.ds(base, WIN), :]).then_inc(dtab_in[s], 16)

            sp.wait_ge(zeros_made, 3)
            sp.dma_start(table_dst[NPAD:NPAD + P, :], sums[0][:, 0:2 * D]).then_inc(tail_stored, 16)
            for g in range(NG):
                sp.wait_ge(copied_act, 4 * (g + 1))
                sp.wait_ge(copied_dve, 3 * (g + 1))
                sp.dma_start(blocks(tsrc_v, g), pq[g % 2][:, :, 0:2 * D]).then_inc(pq_stored[g % 2], 16)
                sp.dma_start(blocks(tdst_v, g), pq[g % 2][:, :, 2 * D:]).then_inc(pq_stored[g % 2], 16)
            sp.wait_ge(index_in, 16 * N_INDEX)

            def store_rows(layer, g, F):
                sp.wait_ge(F.rows_made, F.count(layer, g))
                if layer < 2:
                    sp.dma_start(blocks(table_v[layer], g), new_rows[:, :, :]).then_inc(F.stored[layer], 16)
                elif is_last(g):
                    n = NODES // P - g * GROUP
                    sp.dma_start(out[g * GP:g * GP + n * P, :].rearrange("(b p) d -> p b d", p=P), new_rows[:, 0:n, :])\
                        .then_inc(F.stored[layer], 16)
                    sp.dma_start(out[g * GP + n * P:NODES, :], new_rows[0:NODES % P, n, :]).then_inc(F.stored[layer], 16)
                else:
                    sp.dma_start(out[bass.ds(g * GP, GP), :].rearrange("(b p) d -> p b d", p=P), new_rows[:, :, :])\
                        .then_inc(F.stored[layer], 16)

            def free_rows(layer, g, F):
                sp.wait_ge(F.stored[layer], g * 16 + 16)
                sp.sem_inc(F.rows_free, 1)

            for F in (first_take, retake):
                sp.sem_inc(F.rows_free, 1)
            for layer in range(3):
                for what, i in schedule(sp):
                    if what == "c":
                        store_rows(layer, i, first_take)
                    if what == "d":
                        free_rows(layer, i, first_take)
                    if what != "pair":
                        continue
                    for s in range(2):
                        k = i * 2 + s
                        if is_at_least(i, 1):
                            sp.wait_ge(rows_in[s], (i + layer * HALF) * (16 * EIGHT))
                        load_idx(k, s)
                        if layer == 0:
                            if is_at_least(i, 1):
                                sp.wait_ge(z_ready, k * 4 - 4)
                            load_chunk(k, s)
                with sp.If(any_stray(sp)):
                    with sp.Fori(0, C) as c:
                        with sp.Fori(0, EIGHT) as j:
                            t = c * EIGHT + j
                            sp.wait_ge(f_next, t + (layer * (NT + 1) + 1))
                            sp.dma_start(idx[0][:, 0:1], src_tiles[bass.ds(c, 1), :, bass.ds(j, 1)]
                                         .rearrange("a p j -> (a p) j"), allow_slow_non_contiguous=True).then_inc(f_in, 16)
                            if layer == 0:
                                sp.dma_start(idx[1][:, 0:1], dst_tiles[bass.ds(c, 1), :, bass.ds(j, 1)]
                                             .rearrange("a p j -> (a p) j"), allow_slow_non_contiguous=True).then_inc(f_in, 16)
                                sp.dma_start(edge_sb[0][:, 0:P], edge_T[:, bass.ds(t * P, P)]).then_inc(f_in, 16)
                    with sp.Fori(0, NG - 1) as g:
                        store_rows(layer, g, retake)
                        free_rows(layer, g, retake)
                    sp.wait_ge(retaken, layer + 1)
                store_rows(layer, NG - 1, first_take)
                if layer < 2:
                    free_rows(layer, NG - 1, first_take)
            sp.wait_ge(first_take.stored[2], 16 * (NG + 1))

        @block.gpsimd
        def _(pool):
            pool.iota(iota_i[:, :], pattern=[[1, P]], base=0, channel_multiplier=0).then_inc(ints_made, 1)
            pool.iota(part_i[:, :], pattern=[[0, 1]], base=0, channel_multiplier=1).then_inc(ints_made, 1)
            pool.memset(first_node[:, 0:LEAD], 0).then_inc(first_node_made, 1)
            pool.iota(first_node[:, LEAD:].rearrange("p (g c) -> p g c", g=NG), pattern=[[GP, NG], [0, 2 * PAIRS]],
                      base=0, channel_multiplier=0).then_inc(first_node_made, 1)
            pool.iota(ident_i[:, :], pattern=[[1, P]], base=0, channel_multiplier=-1).then_inc(ints_made, 1)

            def gather(to, table, index):
                return pool.indirect_dma_start(out=to, out_offset=None, in_=table,
                                               in_offset=bass.IndirectOffsetOnAxis(ap=index, axis=0))

            for g in range(NG):
                pool.wait_ge(h_made, g + 1)
                pool.tensor_tensor(blocks(xh, g), blocks(x_sb, g), new_rows[:, :, :], ALU.add).then_inc(xh_made, 1)

            for layer in range(3):
                table = table_src if layer == 0 else tables[layer]
                if layer == 0:
                    first_tables_stored(pool)
                else:
                    pool.wait_ge(first_take.stored[layer - 1], 16 * NG)
                for what, i in schedule(pool):
                    if what != "pair":
                        continue
                    for s in range(2):
                        k = i * 2 + s
                        pool.wait_ge(idx_in[s], i * 16 + 16 * (layer * HALF + 1))
                        if is_at_least(i, 1):
                            if layer == 0:
                                pool.wait_ge(z_added, k * 4 - 4)
                            else:
                                pool.wait_ge(window_done, k + (layer * C - 1))
                        pool.sem_inc(gathers_let, 1)
                        to = rows[s] if layer == 0 else rows1[s]
                        for j in range(EIGHT):
                            gather(to[:, j, :], table, idx[s][:, j:j + 1]).then_inc(rows_in[s], 16)
                with pool.If(any_stray(pool)):
                    with pool.Fori(0, NT) as t:
                        if layer == 0:
                            pool.wait_ge(f_in, t * 48 + 48)
                            pool.sem_inc(gathers_let, 1)
                            gather(rows[0][:, 0, :], table_src, idx[0][:, 0:1]).then_inc(f_rows, 16)
                            gather(rows[1][:, 0, :], table_dst, idx[1][:, 0:1]).then_inc(f_rows, 16)
                        else:
                            pool.wait_ge(f_in, t * 16 + (48 * NT + 16 * (layer - 1) * NT + 16))
                            pool.sem_inc(gathers_let, 1)
                            gather(rows1[0][:, 0, :], table, idx[0][:, 0:1]).then_inc(f_rows, 16)
                    pool.wait_ge(retaken, layer + 1)
                    pool.wait_ge(retake.stored[layer], 16 * (NG - 1))

        @block.scalar
        def _(act):
            def p_square(g):
                act.wait_ge(p_xc, g + 1)
                act.activation(blocks(xh, g), blocks(xc_all, g), ACT.Square).then_inc(p_sq, 1)

            def p_step(g):
                if g + 1 < NG:
                    p_square(g + 1)
                if g < NG:
                    act.wait_ge(p_root_in, g + 1)
                    act.activation(root[:, 0:GROUP], root_in[:, 0:GROUP], ACT.Sqrt).then_inc(p_root, 1)
                    act.wait_ge(h_turned, g + 1)
                    if g >= 2:
                        act.wait_ge(node_prod, (g - 1) * GROUP)
                    act.activation(hT[g % 2][0:D, :, :], ps_t[0:D, 0:GROUP, :], ACT.Copy).then_inc(hT_made, 1)
                if g >= 1:
                    if g >= 3:
                        act.wait_ge(pq_stored[(g - 1) % 2], 32 * ((g - 1) // 2))
                    for j in range(3, GROUP):
                        act.wait_ge(node_prod, (g - 1) * GROUP + j + 1)
                        act.activation(pq[(g - 1) % 2][:, j, :], ps_z[:, j % 4, 0:4 * D], ACT.Copy).then_inc(copied_act, 1)

            p_square(0)
            for g in range(NG + 1):
                p_step(g)

            def logs(k, s):
                act.wait_ge(z_added, k * 4 + 4)
                if is_at_least(k, 2):
                    act.wait_ge(msg_made, k * 2 - 2)
                act.activation(az[s][:, :, :, :], z[s][:, :, :, :], ACT.Abs).then_inc(absd, 1)
                act.wait_ge(absd, k + 1)
                act.activation(az[s][:, :, :, :], az[s][:, :, :, :], ACT.Exp, scale=-1.0).then_inc(expd, 1)
                act.wait_ge(expd, k + 1)
                act.activation(az[s][:, :, :, :], az[s][:, :, :, :], ACT.Ln, bias=1.0).then_inc(logd, 1)

            def gates(k, s):
                act.wait_ge(gate_arg, k + 1)
                act.activation(az[s][:, :, 0, :], az[s][:, :, 0, :], ACT.Exp).then_inc(gate_made, 1)

            def step(k, s):
                if is_chunk(k - 1):
                    logs(k - 1, 1 - s)
                if is_chunk(k - 2):
                    gates(k - 2, s)

            act.preload_act_table_set("natural_log_exp_and_others")
            def stage(layer, g, F):
                n = F.count(layer, g)
                act.wait_ge(F.turned, n)
                if F is retake or is_last(g):
                    act.wait_ge(window_added, (layer + 1) * C)
                else:
                    act.wait_ge(window_added, g * (2 * PAIRS) + (layer * C + 2 * (PAIRS + LEAD) - 3))
                width = D if layer else DX
                act.activation(staged_T[0:width, :], sums_of(layer, g, width), ACT.Copy).then_inc(F.staged, 1)

            def squares(g, F):
                act.wait_ge(F.xc, F.count(0, g))
                act.activation(sq[:, :, :], xc[:, :, :], ACT.Square).then_inc(F.sq, 1)

            def roots(g, F):
                act.wait_ge(F.root_in, F.count(0, g) * 2)
                act.activation(root[:, :], root_in[:, :], ACT.Sqrt).then_inc(F.root, 1)

            def begin_sums(layer, g, F):
                act.wait_ge(F.rows_turned, F.count(layer, g) + 1)
                act.activation(sums_of(layer + 1, g, D), ps_t[0:D, 0:GROUP, :].rearrange("d b n -> d (b n)"), ACT.Copy)\
                    .then_inc(F.t_free, 1)

            def take(layer, g, F, what):
                if what == "a":
                    stage(layer, g, F)
                    if layer == 0:
                        squares(g, F)
                if what == "b" and layer == 0:
                    roots(g, F)
                    act.preload_act_table_set("natural_log_exp_and_others")
                if what == "c" and layer < 2:
                    begin_sums(layer, g, F)

            def retake_all(layer):
                v = first_take.count(layer, NG - 1)
                act.wait_ge(first_take.turned, v)
                with act.Fori(0, NG - 1) as g:
                    for what in "abc":
                        take(layer, g, retake, what)
                act.wait_ge(retaken, layer + 1)

            for F in (first_take, retake):
                act.sem_inc(F.t_free, 1)
            for what, i in schedule(act):
                if what == "pair":
                    for s in range(2):
                        step(i * 2 + s, s)
                else:
                    take(0, i, first_take, what)
            for k in range(C, C + 2):
                step(k, k % 2)

            with act.If(any_stray(act)):
                with act.Fori(0, NT) as t:
                    act.wait_ge(f_z2, t + 1)
                    act.activation(az[0][:, 0, :, :], z[0][:, 0, :, :], ACT.Abs).then_inc(f_abs, 1)
                    act.wait_ge(f_abs, t + 1)
                    act.activation(az[0][:, 0, :, :], az[0][:, 0, :, :], ACT.Exp, scale=-1.0).then_inc(f_exp, 1)
                    act.wait_ge(f_exp, t + 1)
                    act.activation(az[0][:, 0, :, :], az[0][:, 0, :, :], ACT.Ln, bias=1.0).then_inc(f_log, 1)
                    act.wait_ge(f_arg, t + 1)
                    act.activation(az[0][:, 0, 0, :], az[0][:, 0, 0, :], ACT.Exp).then_inc(f_gate, 1)
                retake_all(0)
            for what in "abc":
                take(0, NG - 1, first_take, what)

            for layer in (1, 2):
                with act.Fori(0, NG - 1) as g:
                    for what in "abc":
                        take(layer, g, first_take, what)
                with act.If(any_stray(act)):
                    retake_all(layer)
                for what in "abc":
                    take(layer, NG - 1, first_take, what)

        @block.tensor
        def _(pe):
            pe.wait_ge(consts_made, 3)
            pe.wait_ge(ident_made, 1)
            pe.wait_ge(zeros_made, 3)
            pe.wait_ge(weights_in, 16 * N_WEIGHTS)
            for g in range(NG + 1):
                if g < NG:
                    pe.wait_ge(h_made, g + 1)
                    if g >= 1:
                        pe.wait_ge(hT_made, g)
                    for j in range(GROUP):
                        last = pe.transpose(ps_t[0:D, j, :], new_rows[:, j, :], ident[:, :])
                    last.then_inc(h_turned, 1)
                if g >= 1:
                    pe.wait_ge(hT_made, g)
                    for j in range(GROUP):
                        m = (g - 1) * GROUP + j
                        if j in (4, 5, 6):
                            before = m - 4
                        else:
                            before = (g - 2) * GROUP + (j + 4 if j < 3 else 3)
                        if before >= 0:
                            if before % GROUP < 3:
                                pe.wait_ge(copied_dve, before // GROUP * 3 + before % GROUP + 1)
                            else:
                                pe.wait_ge(copied_act, before // GROUP * 4 + before % GROUP - 2)
                        pe.matmul(ps_z[:, j % 4, 0:4 * D], hT[(g - 1) % 2][:, j, :], w_nodes[:, :], start=True, stop=True)\
                            .then_inc(node_prod, 1)
            pe.wait_ge(copied_act, 4 * NG)
            pe.wait_ge(copied_dve, 3 * NG)
            pe.wait_ge(stray_counted, 2)
            pe.matmul(ps_w[0][0:1, 0:1], ones[:, :], strays[:, 0:1], start=True, stop=False)
            pe.matmul(ps_w[0][0:1, 0:1], ones[:, :], strays[:, 1:2], start=False, stop=True).then_inc(stray_summed, 1)

            def products(k, s, i):
                pe.wait_ge(edge_in[s], i * 16 + 16)
                pe.wait_ge(dtab_in[s], i * 16 + 16)
                pe.wait_ge(hotT_made, k + 1)
                for q in range(4):
                    if is_at_least(k, 1):
                        pe.wait_ge(z_added, k * 4 + (q - 3))
                    for j in (2 * q, 2 * q + 1):
                        to = ps_z[:, q, (j % 2) * 2 * D:(j % 2 + 1) * 2 * D]
                        pe.matmul(to, edge_sb[s][:, j * P:(j + 1) * P], w_edge[:, :], start=True, stop=False)
                        last = pe.matmul(to, hotT[s][:, j * P:(j + 1) * P], dtab[s][:, :], start=False, stop=True)
                    last.then_inc(z_ready, 1)

            def window(K, s, rows_of, width):
                pe.wait_ge(hot_made, K + 1)
                if is_at_least(K, 2):
                    pe.wait_ge(window_added, K - 1)
                for j in range(EIGHT):
                    last = pe.matmul(ps_w[s][0:width, 0:WIN], rows_of[:, j, :], hot[s][:, j, :],
                                     start=(j == 0), stop=(j == EIGHT - 1))
                last.then_inc(window_done, 1)

            def first_layer_step(k, s, i):
                if is_chunk(k - 3):
                    pe.wait_ge(msg_made, k * 2 - 4)
                    window(k - 3, 1 - s, msg[1 - s], DX)
                if is_chunk(k):
                    products(k, s, i)

            def stray_windows(layer, t):
                with pe.Fori(0, NB) as w:
                    n = t * NB + w
                    pe.wait_ge(f_hot, n + (layer * NT * NB + 1))
                    pe.matmul(ps_w[0][0:DX, 0:P], msg_one[:, :], hot_one, start=True, stop=True).then_inc(f_sum, 1)

            def turn_sums(layer, g, F):
                n = F.count(layer, g)
                pe.wait_ge(F.staged, n)
                pe.wait_ge(F.t_free, n)
                for j in range(GROUP):
                    if layer == 0:
                        last = pe.transpose(ps_t[:, j, 0:DX], staged_T[0:DX, j * P:(j + 1) * P], ident[0:DX, 0:DX])
                    else:
                        last = pe.matmul(ps_t[:, j, 0:D], staged_T[0:D, j * P:(j + 1) * P], w_gcn[layer][:, :],
                                         start=True, stop=True)
                last.then_inc(F.turned, 1)

            def turn_rows(layer, g, F):
                pe.wait_ge(F.rows_made, F.count(layer, g))
                for j in range(GROUP):
                    last = pe.transpose(ps_t[0:D, j, :], new_rows[:, j, :], ident[:, :])
                last.then_inc(F.rows_turned, 1)

            def take(layer, g, F, what):
                if what == "a":
                    turn_sums(layer, g, F)
                if what == "c" and layer < 2:
                    turn_rows(layer, g, F)

            def retake_all(layer):
                pe.wait_ge(first_take.t_free, first_take.count(layer, NG - 1))
                with pe.Fori(0, NG - 1) as g:
                    for what in "abc":
                        take(layer, g, retake, what)
                pe.wait_ge(retaken, layer + 1)

            for F in (first_take, retake):
                pe.sem_inc(F.turned, 1)
                pe.sem_inc(F.rows_turned, 1)
            pe.wait_ge(flag_ready, 1)
            for what, i in schedule(pe):
                if what == "pair":
                    for s in range(2):
                        first_layer_step(i * 2 + s, s, i)
                else:
                    take(0, i, first_take, what)
            for k in range(C, C + 3):
                first_layer_step(k, k % 2, None)
            with pe.If(any_stray(pe)):
                with pe.Fori(0, NT) as t:
                    pe.wait_ge(f_in, t * 48 + 48)
                    pe.matmul(ps_z[:, 0, 0:2 * D], edge_sb[0][:, 0:P], w_edge[:, :], start=True, stop=True)\
                        .then_inc(f_z, 1)
                    stray_windows(0, t)
                retake_all(0)
            for what in "abc":
                take(0, NG - 1, first_take, what)

            for layer in (1, 2):
                for what, i in schedule(pe):
                    if what == "pair":
                        for s in range(2):
                            pe.wait_ge(rows_in[s], i * (16 * EIGHT) + (layer * HALF + 1) * 16 * EIGHT)
                            window(i * 2 + (layer * C + s), s, rows1[s], D)
                    else:
                        take(layer, i, first_take, what)
                with pe.If(any_stray(pe)):
                    with pe.Fori(0, NT) as t:
                        stray_windows(layer, t)
                    retake_all(layer)
                for what in "abc":
                    take(layer, NG - 1, first_take, what)

        @block.vector
        def _(dve):
            TT, TS = dve.tensor_tensor, dve.tensor_scalar
            for s in range(2):
                dve.memset(rows[s][D:D + 1, :, :], 1.0).then_inc(zeros_made, 1)
            dve.memset(sums[0][:, :], 0.0).then_inc(zeros_made, 1)
            dve.memset(sums[1][:, NPAD:], 0.0)
            dve.memset(ones[:, :], 1.0).then_inc(consts_made, 1)
            for s in range(2):
                dve.memset(msg[s][:, :, D:D + 1], 1.0)
            dve.memset(msg_one[:, :], 0.0)
            dve.wait_ge(ints_made, 3)
            dve.tensor_copy(iota_f[:, :], iota_i[:, :]).then_inc(consts_made, 1)
            dve.tensor_copy(part_f[:, :], part_i[:, :]).then_inc(consts_made, 1)
            TS(ident[:, :], ident_i[:, :], 0.0, None, ALU.is_equal).then_inc(ident_made, 1)
            dve.wait_ge(consts_made, 3)

            def p_center(g):
                dve.wait_ge(x_in[g], 16)
                dve.reduce_sum(total[:, :], blocks(x_sb, g), X).then_inc(p_total, 1)
                dve.wait_ge(p_total, g + 1)
                TS(nmean[:, :], total[:, :], -1.0 / D, None, ALU.mult).then_inc(p_nmean, 1)
                dve.wait_ge(p_nmean, g + 1)
                TT(blocks(xc_all, g), blocks(x_sb, g), along(nmean[:, :], D), ALU.add).then_inc(p_xc, 1)
                dve.wait_ge(p_xc, g + 1)

            def p_rows(g):
                dve.wait_ge(p_sq, g + 1)
                dve.reduce_sum(var[:, :], blocks(xh, g), X).then_inc(p_var, 1)
                dve.wait_ge(p_var, g + 1)
                TS(root_in[:, 0:GROUP], var[:, :], 1.0 / D, EPS, ALU.mult, ALU.add).then_inc(p_root_in, 1)
                dve.wait_ge(p_root, g + 1)
                dve.reciprocal(rroot[:, 0:GROUP], root[:, 0:GROUP]).then_inc(p_rroot, 1)
                dve.wait_ge(p_rroot, g + 1)
                if g >= 1:
                    dve.wait_ge(h_turned, g)
                    dve.wait_ge(xh_made, g)
                relu_times(new_rows[:, :, :], blocks(xc_all, g), rroot[:, 0:GROUP]).then_inc(h_made, 1)
                dve.wait_ge(h_made, g + 1)

            def p_copy(g):
                if g >= 2:
                    dve.wait_ge(pq_stored[g % 2], 32 * (g // 2))
                for j in range(3):
                    dve.wait_ge(node_prod, g * GROUP + j + 1)
                    dve.tensor_copy(pq[g % 2][:, j, :], ps_z[:, j % 4, 0:4 * D]).then_inc(copied_dve, 1)

            def relu_times(out, a, scale):
                return dve.scalar_tensor_tensor(out=out, in0=a, scalar=0.0, in1=along(scale, D), op0=ALU.max, op1=ALU.mult)

            p_center(0)
            for g in range(NG + 1):
                if g + 1 < NG:
                    p_center(g + 1)
                if g < NG:
                    p_rows(g)
                if g >= 1:
                    p_copy(g - 1)

            dve.wait_ge(index_in, 16 * N_INDEX)
            TS(window_node[:, :], base_b[:, :], part_f[:, :], None, ALU.add)
            TT(dst_rel[:, :, :], dst_i[:, :, :], along(base_b[:, :], EIGHT), ALU.subtract).then_inc(rel_made, 1)
            dve.wait_ge(first_node_made, 2)
            TT(late[:, :, :], dst_i[:, :, :], along(first_node[:, 0:C], EIGHT), ALU.is_lt).then_inc(late_made, 1)
            dve.wait_ge(rel_made, 1)
            TS(stray[:, :, :], dst_rel[:, :, :], float(WIN), None, ALU.is_ge).then_inc(inside_made, 1)
            dve.wait_ge(inside_made, 1)
            dve.scalar_tensor_tensor(out=stray[:, :, :], in0=dst_rel[:, :, :], scalar=0.0, in1=stray[:, :, :],
                                     op0=ALU.is_lt, op1=ALU.add).then_inc(stray_made, 1)
            dve.wait_ge(late_made, 1)
            dve.reduce_sum(strays[:, 1:2], late[:, :, :].rearrange("p c j -> p (c j)"), X).then_inc(stray_counted, 1)
            dve.wait_ge(stray_made, 1)
            dve.reduce_sum(strays[:, 0:1], stray[:, :, :].rearrange("p c j -> p (c j)"), X).then_inc(stray_counted, 1)
            dve.wait_ge(stray_summed, 1)
            dve.tensor_copy(flag[:, :], ps_w[0][0:1, 0:1]).then_inc(flag_ready, 1)

            def targets_hot(k, s, i):
                dve.wait_ge(dstw_in[s], i * 16 + 16)
                TS(hotT[s][:, :], dstw[s][:, :], window_node[0:WIN, bass.ds(k, 1)], None, ALU.is_equal)\
                    .then_inc(hotT_made, 1)

            def add_sources(k, s, i):
                dve.wait_ge(rows_in[s], i * (16 * EIGHT) + 16 * EIGHT)
                if is_at_least(k, 2):
                    dve.wait_ge(plus_made, k - 1)
                for q in range(4):
                    dve.wait_ge(z_ready, k * 4 + (q + 1))
                    TT(z[s][:, 2 * q:2 * q + 2, :, :].rearrange("p a b d -> p (a b d)"), ps_z[:, q, 0:4 * D],
                       rows[s][:, 2 * q:2 * q + 2, :].rearrange("p a d -> p (a d)"), ALU.add).then_inc(z_added, 1)

            def sum_args(k, s):
                dve.wait_ge(logd, k + 1)
                dve.scalar_tensor_tensor(out=az[s][:, :, 0, :], in0=z[s][:, :, 0, :], scalar=0.0, in1=az[s][:, :, 0, :],
                                         op0=ALU.min, op1=ALU.subtract).then_inc(gate_arg, 1)
                dve.scalar_tensor_tensor(out=az[s][:, :, 1, :], in0=z[s][:, :, 1, :], scalar=0.0, in1=az[s][:, :, 1, :],
                                         op0=ALU.max, op1=ALU.add).then_inc(plus_made, 1)

            def messages(k, s):
                dve.wait_ge(gate_made, k + 1)
                dve.wait_ge(plus_made, k + 1)
                TT(msg[s][:, :, 0:D], az[s][:, :, 0, :], az[s][:, :, 1, :], ALU.mult).then_inc(msg_made, 1)
                dve.tensor_copy(msg[s][:, :, D + 1:DX].rearrange("p j a -> p (j a)"),
                                ew_sb[:, bass.ds(k, 1), :].rearrange("p a j -> p (a j)")).then_inc(msg_made, 1)

            def targets(k, s, K, weighted):
                rel_k = dst_rel[:, bass.ds(k, 1), :].rearrange("p a j -> p (a j)")
                to = hoti[s] if weighted else hot[s]
                if weighted:
                    dve.wait_ge(hot_made, K - 1)
                made = TT(to[:, :, :], across(iota_f[:, 0:WIN], EIGHT), along(rel_k, WIN), ALU.is_equal)
                if not weighted:
                    made.then_inc(hot_made, 1)
                    return
                made.then_inc(equal_made, 1)
                dve.wait_ge(equal_made, K - C + 1)
                TT(hot[s][:, :, :], hoti[s][:, :, :], along(ew_sb[:, bass.ds(k, 1), :].rearrange("p a j -> p (a j)"), WIN),
                   ALU.mult).then_inc(hot_made, 1)

            def add_window(k, s, K, width, layer=0):
                base = dve.value_load(base_b[0:1, bass.ds(k, 1)], min_val=0, max_val=NPAD - 1)
                at = sums[layer % 2][0:width, bass.ds(base, WIN)]
                dve.wait_ge(window_done, K + 1)
                if is_at_least(K, 1):
                    dve.wait_ge(window_added, K)
                TT(at, at, ps_w[s][0:width, 0:WIN], ALU.add).then_inc(window_added, 1)

            def first_layer_step(k, s, i):
                if is_chunk(k):
                    targets_hot(k, s, i)
                if is_chunk(k - 3):
                    messages(k - 3, 1 - s)
                if is_chunk(k - 1):
                    add_sources(k - 1, 1 - s, i if s else i - 1)
                if is_chunk(k - 2):
                    sum_args(k - 2, s)
                if is_chunk(k - 3):
                    add_window(k - 3, 1 - s, k - 3, DX)
                if is_chunk(k - 1):
                    targets(k - 1, 1 - s, k - 1, False)

            def strays_of(layer):
                dve.drain().then_inc(f_next, 1)
                with dve.Fori(0, C) as c:
                    with dve.Fori(0, EIGHT) as j:
                        t = c * EIGHT + j
                        T = t + layer * NT
                        stray_t = stray[:, bass.ds(c, 1), bass.ds(j, 1)].rearrange("p a b -> p (a b)")
                        ew_t = ew_sb[:, bass.ds(c, 1), bass.ds(j, 1)].rearrange("p a b -> p (a b)")
                        dst_t = dst_i[:, bass.ds(c, 1), bass.ds(j, 1)].rearrange("p a b -> p (a b)")
                        if layer == 0:
                            zt, at = z[0][:, 0, :, :], az[0][:, 0, :, :]
                            flat = zt.rearrange("p b d -> p (b d)")
                            dve.wait_ge(f_rows, t * 32 + 32)
                            dve.wait_ge(f_z, t + 1)
                            TT(flat, ps_z[:, 0, 0:2 * D], rows[0][:, 0, :], ALU.add).then_inc(f_z1, 1)
                            dve.wait_ge(f_z1, t + 1)
                            TT(flat, flat, rows[1][:, 0, :], ALU.add).then_inc(f_z2, 1)
                            dve.wait_ge(f_z2, t + 1)
                            dve.wait_ge(f_log, t + 1)
                            dve.scalar_tensor_tensor(out=at[:, 0, :], in0=zt[:, 0, :], scalar=0.0, in1=at[:, 0, :],
                                                     op0=ALU.min, op1=ALU.subtract).then_inc(f_arg, 1)
                            dve.scalar_tensor_tensor(out=at[:, 1, :], in0=zt[:, 1, :], scalar=0.0, in1=at[:, 1, :],
                                                     op0=ALU.max, op1=ALU.add).then_inc(f_plus, 1)
                            dve.tensor_copy(msg[0][:, 0, D + 1:DX], ew_t).then_inc(f_prod, 1)
                            dve.wait_ge(f_plus, t + 1)
                            dve.wait_ge(f_gate, t + 1)
                            TT(msg[0][:, 0, 0:D], at[:, 0, :], at[:, 1, :], ALU.mult).then_inc(f_prod, 1)
                            dve.wait_ge(f_prod, t * 2 + 2)
                            TS(msg_one[:, :], msg[0][:, 0, :], stray_t, None, ALU.mult).then_inc(f_msg, 1)
                        else:
                            dve.wait_ge(f_rows, t * 16 + (32 * NT + 16 * (layer - 1) * NT + 16))
                            TS(msg_one[:, 0:D], rows1[0][:, 0, :], stray_t, ew_t, ALU.mult, ALU.mult).then_inc(f_msg, 1)
                        dve.tensor_copy(rel[:, :], dst_t).then_inc(f_rel, 1)
                        with dve.Fori(0, NB) as w:
                            n = T * NB + w
                            dve.wait_ge(f_msg, T + 1)
                            dve.wait_ge(f_rel, n + T + 1)
                            TS(hot_one, iota_f[:, :], rel[:, :], None, ALU.is_equal).then_inc(f_hot, 1)
                            dve.wait_ge(f_hot, n + 1)
                            TS(rel[:, :], rel[:, :], float(-P), None, ALU.add).then_inc(f_rel, 1)
                            at_w = sums[layer % 2][0:DX, bass.ds(w * P, P)]
                            dve.wait_ge(f_sum, n + 1)
                            TT(at_w, at_w, ps_w[0][0:DX, 0:P], ALU.add).then_inc(f_acc, 1)
                            dve.wait_ge(f_acc, n + 1)
                        dve.drain().then_inc(f_next, 1)

            def center(g, F):
                n = F.count(0, g)
                dve.wait_ge(F.turned, n + 1)
                TS(cnt[:, :], ps_t[:, 0:GROUP, D], 1.0, None, ALU.max).then_inc(F.cnt, 1)
                TS(dpos[:, :], ps_t[:, 0:GROUP, D + 1], 1.0, 0.0, ALU.add, ALU.is_gt).then_inc(F.dpos, 1)
                TS(root_in[:, GROUP:], ps_t[:, 0:GROUP, D + 1], 1.0, 1e-30, ALU.add, ALU.max).then_inc(F.root_in, 1)
                dve.wait_ge(F.cnt, n)
                dve.reciprocal(rcnt[:, :], cnt[:, :]).then_inc(F.rcnt, 1)
                dve.wait_ge(F.rcnt, n)
                TT(sq[:, :, :], ps_t[:, 0:GROUP, 0:D], along(rcnt[:, :], D), ALU.mult).then_inc(F.hnew, 1)
                dve.wait_ge(F.hnew, n)
                TT(blocks(x_sb, g), sq[:, :, :], blocks(xh, g), ALU.add).then_inc(F.x1, 1)
                dve.wait_ge(F.x1, n)
                dve.sem_inc(sums_let, 1)
                dve.reduce_sum(total[:, :], blocks(x_sb, g), X).then_inc(F.total, 1)
                dve.wait_ge(F.total, n)
                TS(nmean[:, :], total[:, :], -1.0 / D, None, ALU.mult).then_inc(F.nmean, 1)
                dve.wait_ge(F.nmean, n)
                TT(xc[:, :, :], blocks(x_sb, g), along(nmean[:, :], D), ALU.add).then_inc(F.xc, 1)

            def free_to_write(n, F):
                dve.wait_ge(F.rows_free, n)
                dve.wait_ge(F.rows_turned, n)

            def rows_first(g, F):
                n = F.count(0, g)
                dve.wait_ge(F.sq, n)
                dve.reduce_sum(var[:, :], sq[:, :, :], X).then_inc(F.var, 1)
                dve.wait_ge(F.var, n)
                TS(root_in[:, 0:GROUP], var[:, :], 1.0 / D, EPS, ALU.mult, ALU.add).then_inc(F.root_in, 1)
                dve.wait_ge(F.root, n)
                dve.reciprocal(rroot[:, :], root[:, :]).then_inc(F.rroot, 1)
                dve.wait_ge(F.rroot, n)
                dve.wait_ge(F.dpos, n)
                TT(columns(dinv, g), rroot[:, GROUP:], dpos[:, :], ALU.mult).then_inc(F.dinv, 1)
                dve.wait_ge(F.dinv, n)
                TT(rd[:, :], rroot[:, 0:GROUP], columns(dinv, g), ALU.mult).then_inc(F.rd, 1)
                dve.wait_ge(F.rd, n)
                free_to_write(n, F)
                relu_times(new_rows[:, :, :], xc[:, :, :], rd[:, :]).then_inc(F.rows_made, 1)

            def rows_gcn(layer, g, F):
                n = F.count(layer, g)
                m = n - F.per_layer
                dve.wait_ge(F.turned, n + 1)
                scaled = TT(xc[:, :, :], ps_t[:, 0:GROUP, 0:D], along(columns(dinv, g), D), ALU.mult)
                scaled.then_inc(F.scaled, 1)
                dve.wait_ge(F.scaled, m)
                if layer == 2:
                    dve.sem_inc(F.t_free, 1)
                TT(sq[:, :, :], xc[:, :, :], across(b_gcn[layer][:, :], GROUP), ALU.add).then_inc(F.biased, 1)
                dve.wait_ge(F.biased, m)
                if layer == 1:
                    free_to_write(n, F)
                    relu_times(new_rows[:, :, :], sq[:, :, :], columns(dinv, g)).then_inc(F.rows_made, 1)
                else:
                    dve.wait_ge(F.rows_free, n)
                    dve.scalar_tensor_tensor(out=new_rows[:, :, :], in0=sq[:, :, :], scalar=0.0, in1=blocks(x_sb, g),
                                             op0=ALU.max, op1=ALU.add).then_inc(F.rows_made, 1)

            def take(layer, g, F, what):
                if what == "a":
                    if layer == 0:
                        center(g, F)
                    else:
                        rows_gcn(layer, g, F)
                if what == "b" and layer == 0:
                    rows_first(g, F)

            def retake_all(layer):
                v = first_take.count(layer, NG - 1)
                dve.wait_ge(first_take.rows_free, v)
                dve.wait_ge(first_take.t_free, v)
                with dve.Fori(0, NG - 1) as g:
                    for what in "ab":
                        take(layer, g, retake, what)
                v = retake.count(layer, NG - 1)
                dve.wait_ge(retake.rows_free, v)
                dve.wait_ge(retake.t_free, v)
                dve.drain().then_inc(retaken, 1)

            dve.wait_ge(xh_made, NG)
            dve.wait_ge(h_turned, NG)
            for what, i in schedule(dve):
                if what == "pair":
                    for s in range(2):
                        first_layer_step(i * 2 + s, s, i)
                else:
                    take(0, i, first_take, what)
            for k in range(C, C + 3):
                first_layer_step(k, k % 2, k // 2)
            dve.wait_ge(window_added, C)
            with dve.If(any_stray(dve)):
                strays_of(0)
                retake_all(0)
            for what in "ab":
                take(0, NG - 1, first_take, what)

            for layer in (1, 2):
                dve.wait_ge(first_take.t_free, layer * NG + 1)
                for what, i in schedule(dve):
                    if what != "pair":
                        take(layer, i, first_take, what)
                        continue
                    for s in range(2):
                        k = i * 2 + s
                        targets(k, s, k + layer * C, True)
                        if is_chunk(k - 1):
                            add_window(k - 1, 1 - s, k + (layer * C - 1), D, layer)
                add_window(C - 1, 1, (layer + 1) * C - 1, D, layer)
                dve.wait_ge(window_added, (layer + 1) * C)
                with dve.If(any_stray(dve)):
                    strays_of(layer)
                    retake_all(layer)
                take(layer, NG - 1, first_take, "a")


def kernel(x, src, dst, edge_attr_64, edge_weight, L0_gnn_W_e, L0_gnn_b_e, L0_gnn_W_n, L0_gnn_b_n,
           L1_gnn_W1, L1_gnn_b1, L1_gnn_W2, L1_gnn_b2):
    import numpy as np
    import concourse.bacc as bacc
    from concourse.bass_utils import run_bass_kernel_spmd as run

    nodes, edges = x.shape[0], src.shape[0]
    node_pad = -nodes % (P * GROUP)
    tile_pad = -edges % (2 * P * EIGHT)
    chunks = (edges + tile_pad) // (P * EIGHT)
    x = np.pad(np.asarray(x), ((0, node_pad), (0, 0)))
    src = np.pad(np.asarray(src), (0, tile_pad)).reshape(chunks, EIGHT, P)
    dst = np.pad(np.asarray(dst), (0, tile_pad), constant_values=nodes).reshape(chunks, EIGHT, P)
    ew = np.pad(np.asarray(edge_weight), (0, tile_pad)).reshape(chunks, EIGHT, P)
    edge_T = np.pad(np.asarray(edge_attr_64), ((0, tile_pad), (0, 0))).T
    W_e, W_n = np.asarray(L0_gnn_W_e), np.asarray(L0_gnn_W_n)
    both = np.concatenate([W_e, W_n], axis=1)
    bias = np.concatenate([np.zeros_like(both[0]), np.asarray(L0_gnn_b_e), np.asarray(L0_gnn_b_n)])
    arrays = {
        "x": x, "src_tiles": src.transpose(0, 2, 1), 
        "dst_rows": dst.reshape(chunks, EIGHT * P), "dst_cols": dst.transpose(2, 0, 1), "dst_tiles": dst.transpose(0, 2, 1),
        "ew_cols": ew.transpose(2, 0, 1), "chunk_base": dst[:, 0, 0], "edge_T": edge_T,
        "W_nodes": np.concatenate([np.concatenate([both[0:D], both[D:2 * D]], axis=1), bias[None]]), "W_edge": both[2 * D:],
        "W1": np.asarray(L1_gnn_W1), "b1": np.asarray(L1_gnn_b1), "W2": np.asarray(L1_gnn_W2), "b2": np.asarray(L1_gnn_b2),
    }
    nc = bacc.Bacc("TRN2", target_bir_lowering=False, num_devices=1)
    args, feeds = {}, {}
    for name, a in arrays.items():
        feeds[f"in_{name}"] = a = np.ascontiguousarray(a)
        args[name] = nc.dram_tensor(f"in_{name}", a.shape, mybir.dt.from_np(a.dtype), kind="ExternalInput").ap()
    args["out"] = nc.dram_tensor("out_0", (nodes, D), F32, kind="ExternalOutput").ap()
    gnn_program(nc, **args)
    return run(nc, [feeds], core_ids=[0]).results[0]["out_0"]
```

```python
from contextlib import ExitStack

import concourse.bass as bass
from concourse import mybir

F32 = mybir.dt.float32
I32 = mybir.dt.int32
ALU = mybir.AluOpType
ACT = mybir.ActivationFunctionType
X = mybir.AxisListType.X

P = 128
D = 96
DE = 64
EPS = 1e-5
WIN = 64
EIGHT = 8
FOUR = EIGHT // 2
GROUP = 7
LEAD = 3
BEHIND = 4
SPLIT = 3
DX = D + 2


def gnn_program(nc, x, src_tiles, dst_rows, dst_cols, dst_tiles, ew_cols, window_base, edge_T,
                W_nodes, W_edge, W1, b1, W2, b2, out, spare):
    NODES = out.shape[0]
    NPAD = x.shape[0]
    NB = NPAD // P
    NG = NB // GROUP
    C = src_tiles.shape[0]
    NT = C * EIGHT
    HALF = C // 2
    PAIRS = HALF // NG
    CE = EIGHT * P
    GP = GROUP * P
    assert DE + WIN == P
    assert NB % GROUP == 0 and C % 2 == 0 and HALF % NG == 0 and PAIRS >= LEAD + 4 and NG >= 2

    def schedule(eng, layer):
        def pair(i):
            yield "chunk", (i, 0)
            yield "chunk", (i, 1)

        for i in range(2):
            yield from pair(i)
        with eng.Fori(2, PAIRS - 1) as i:
            yield from pair(i)
        with eng.Fori(1, NG) as g:
            with eng.Fori(0, LEAD + 1) as i:
                yield from pair(g * PAIRS + i - 1)
            yield "a", g - 1
            yield from pair(g * PAIRS + LEAD)
            yield "b", g - 1
            yield from pair(g * PAIRS + (LEAD + 1))
            yield "c", g - 1
            even, odd = pair(g * PAIRS + (LEAD + 2))
            yield even
            yield "d", g - 1
            yield odd
            yield "e", g - 1
            if LEAD + 3 < PAIRS - 1:
                with eng.Fori(LEAD + 3, PAIRS - 1) as i:
                    yield from pair(g * PAIRS + i)
            yield "f", g - 1
        even, odd = pair(HALF - 1)
        for event in ("a", even, "b", odd) if layer == 0 else ("a", "b", even, "e", odd, "f"):
            yield event if isinstance(event, tuple) else (event, NG - 1)

    def is_at_least(k, least):
        return not isinstance(k, int) or k >= least

    def is_chunk(k):
        return not isinstance(k, int) or 0 <= k < C

    table_src = nc.dram_tensor("table_src", [NPAD, 2 * D], F32).ap()
    table_dst = nc.dram_tensor("table_dst", [NPAD + P, 2 * D], F32).ap()
    tables = [None, nc.dram_tensor("table_1", [NPAD, D], F32).ap(), nc.dram_tensor("table_2", [NPAD, D], F32).ap()]

    with ExitStack() as ctx:
        def sb(name, shape, dt=F32):
            return ctx.enter_context(nc.sbuf_tensor(name, shape, dt))

        def sem(name):
            return ctx.enter_context(nc.semaphore(name))

        x_sb = sb("x_sb", [P, NB, D])
        xh = sb("xh", [P, NB, D])
        sums = [sb(f"sums{n}", [P, NPAD + P]) for n in range(2)]
        dinv = sb("dinv", [P, NB])
        dst_rel = sb("dst_rel", [P, C, EIGHT])
        dst_i = sb("dst_i", [P, C, EIGHT], I32)
        ew_sb = sb("ew_sb", [P, C, EIGHT])
        stray = sb("stray", [P, C, EIGHT])
        base_b = sb("base_b", [P, 2 * C], I32)
        window_node = sb("window_node", [P, 2 * C])
        iota_i = sb("iota_i", [P, P], I32)
        iota_f = sb("iota_f", [P, P])
        part_i = sb("part_i", [P, 1], I32)
        part_f = sb("part_f", [P, 1])
        ident_i = sb("ident_i", [P, P], I32)
        ident = sb("ident", [P, P])
        ones = sb("ones", [P, 1])
        w_nodes = sb("w_nodes", [D + 1, 4 * D])
        w_gcn = [None, sb("w1_sb", [D, D]), sb("w2_sb", [D, D])]
        b_gcn = [None, sb("b1_sb", [P, D]), sb("b2_sb", [P, D])]
        AHEAD = 2 * LEAD - BEHIND
        first_node = sb("first_node", [P, C + AHEAD], I32)
        strays = sb("strays", [P, 2])
        flag = sb("flag", [1, 1], I32)
        rel = sb("rel", [P, 1])
        msg_one = sb("msg_one", [P, DX])
        total = sb("total", [P, GROUP])
        nmean = sb("nmean", [P, GROUP])
        xc = sb("xc", [P, GROUP, D])
        sq = sb("sq", [P, GROUP, D])
        var = sb("var", [P, GROUP])
        root_in = sb("root_in", [P, 2 * GROUP])
        root = sb("root", [P, 2 * GROUP])
        rroot = sb("rroot", [P, 2 * GROUP])
        staged_T = sb("staged_T", [P, GP])
        new_rows = sb("new_rows", [P, GROUP, D])
        cnt = sb("cnt", [P, GROUP])
        rcnt = sb("rcnt", [P, GROUP])
        dpos = sb("dpos", [P, GROUP])
        rd = sb("rd", [P, GROUP])
        idx = [sb(f"idx{s}", [P, EIGHT], I32) for s in range(2)]
        rows = [sb(f"rows{s}", [P, EIGHT, 2 * D]) for s in range(2)]
        rows1 = [rows[s][:, :, :].rearrange("p a d -> p (a d)")[:, 0:EIGHT * D].rearrange("p (a d) -> p a d", d=D)
                 for s in range(2)]
        mixed = [sb(f"mixed{s}", [P, CE]) for s in range(2)]
        edge_sb = [m[0:DE, :] for m in mixed]
        hotT = [m[DE:P, :] for m in mixed]
        w_mixed = [sb(f"w_mixed{s}", [P, 2, 2 * D]) for s in range(2)]
        dstw = [sb(f"dstw{s}", [P, CE], I32)[DE:P, :] for s in range(2)]
        hot = [sb(f"hot{s}", [P, EIGHT, WIN]) for s in range(2)]
        hoti = [m[:, 0:EIGHT * WIN].rearrange("p (j w) -> p j w", w=WIN) for m in mixed]
        ZW = EIGHT * 2 * D
        work = sb("work", [P, 6 * ZW])
        z, az, gp = ([work[:, (2 * n + s) * ZW:(2 * n + s + 1) * ZW].rearrange("p (j h d) -> p j h d", h=2, d=D)
                      for s in range(2)] for n in range(3))
        late = gp[1].rearrange("p j h d -> p (j h d)")[:, 0:C * EIGHT].rearrange("p (c j) -> p c j", j=EIGHT)
        PQ = 4
        pq = [work[:, s * GROUP * 2 * D:(s + 1) * GROUP * 2 * D].rearrange("p (b n) -> p b n", n=2 * D) for s in range(PQ)]
        hT = sums[1][0:D + 1, 0:NPAD].rearrange("p (b n) -> p b n", n=P)
        p_xc_t = [xc, sq]
        msg = [sb(f"msg{s}", [P, EIGHT, DX]) for s in range(2)]
        hot_one = hot[0][:, :, :].rearrange("p j w -> p (j w)")[:, 0:P]
        ps_z = ctx.enter_context(nc.psum_tensor("ps_z", [P, 4, 512], F32))
        ps_w = [ctx.enter_context(nc.psum_tensor(f"ps_w{s}", [P, 512], F32)) for s in range(2)]
        ps_t = ctx.enter_context(nc.psum_tensor("ps_t", [P, 8, P], F32))

        x_in = [sem(f"x_in{g}") for g in range(NG)]
        w_nodes_in, weights_in, index_in = sem("w_nodes_in"), sem("weights_in"), sem("index_in")
        idx_in = [sem(f"idx_in{s}") for s in range(2)]
        edge_in = [sem(f"edge_in{s}") for s in range(2)]
        window_in = [sem(f"window_in{s}") for s in range(2)]
        dstw_in = [sem(f"dstw_in{s}") for s in range(2)]
        rows_in = [sem(f"rows_in{s}") for s in range(2)]
        tail_stored = sem("tail_stored")
        pq_stored = [sem(f"pq{s}_stored") for s in range(PQ)]
        gathers_let, sums_let = sem("gathers_let"), sem("sums_let")
        ints_made, consts_made, ident_made, zeros_made, ones_made = (
            sem(f"{n}_made") for n in "ints consts ident zeros ones".split())
        rel_made, inside_made, stray_made = sem("rel_made"), sem("inside_made"), sem("stray_made")
        stray_counted = sem("stray_counted")
        first_node_made = sem("first_node_made")
        late_made, stray_summed, flag_ready = sem("late_made"), sem("stray_summed"), sem("flag_ready")
        p_total, p_nmean, p_xc, p_sq, p_var, p_root_in, p_root, p_rroot = (
            sem(f"p_{n}") for n in "total nmean xc sq var root_in root rroot".split())
        h_made, xh_made, h_turned, hT_made = sem("h_made"), sem("xh_made"), sem("h_turned"), sem("hT_made")
        node_prod, copied = sem("node_prod"), [sem(f"copied{q}") for q in range(4)]
        hotT_made, z_ready, z_added = sem("hotT_made"), sem("z_ready"), sem("z_added")
        absd, expd, logd = sem("absd"), sem("expd"), sem("logd")
        gate_arg, gate_made, plus_made, msg_made = sem("gate_arg"), sem("gate_made"), sem("plus_made"), sem("msg_made")
        equal_made, hot_made = sem("equal_made"), sem("hot_made")
        window_done, window_added = sem("window_done"), sem("window_added")
        class Taking:
            def __init__(self, name, per_layer):
                self.per_layer = per_layer
                (self.staged, self.turned, self.rows_turned, self.t_free, self.rows_free, self.rows_made, self.cnt, self.rcnt,
                 self.dpos, self.hnew, self.x1, self.total, self.nmean, self.xc, self.sq, self.var, self.root_in, self.root,
                 self.rroot, self.dinv, self.rd, self.scaled, self.biased) = (sem(f"{name}_{what}") for what in (
                     "staged turned rows_turned t_free rows_free rows_made cnt rcnt dpos hnew x1 total nmean xc sq var "
                     "root_in root rroot dinv rd scaled biased").split())
                self.stored = [sem(f"{name}_stored{n}") for n in range(1, 4)]

            def count(self, layer, g):
                return g + (layer * self.per_layer + 1)

        first_take, retake = Taking("take", NG + 1), Taking("retake", NG)
        strays_added, retaken = sem("strays_added"), sem("retaken")
        f_next, f_in, f_rows, f_z, f_z1, f_z2 = (sem(f"f_{n}") for n in "next in rows z z1 z2".split())
        f_abs, f_exp, f_log, f_arg, f_plus, f_gate = (sem(f"f_{n}") for n in "abs exp log arg plus gate".split())
        f_prod, f_msg, f_rel, f_hot, f_sum, f_acc = (sem(f"f_{n}") for n in "prod msg rel hot sum acc".split())

        N_WEIGHTS, N_INDEX = 8, 3

        def along(a, n):
            return a.unsqueeze(2).to_broadcast([a.shape[0], a.shape[1], n])

        def across(a, k):
            return a.unsqueeze(1).to_broadcast([a.shape[0], k, a.shape[1]])

        def halves(a):
            return a[:, :, :].rearrange("p c (b j) -> p (c b) j", j=FOUR)

        def blocks(a, g):
            return a[:, g * GROUP:(g + 1) * GROUP, :]

        def is_last(g):
            return isinstance(g, int) and g == NG - 1

        def blocks_in(g):
            if isinstance(g, int) and g >= NG - 1:
                return SPLIT if g == NG - 1 else GROUP - SPLIT
            return GROUP

        def first_block(g):
            return (NG - 1) * GROUP + SPLIT if isinstance(g, int) and g == NG else g * GROUP

        OVER = (NODES - first_block(NG) * P) % blocks_in(NG)

        def taken(a, g):
            return a[:, bass.ds(first_block(g), blocks_in(g)), :]

        def columns(a, g):
            return a[:, bass.ds(first_block(g), blocks_in(g))]

        def sums_of(layer, g, n):
            return sums[layer % 2][0:n, bass.ds(first_block(g) * P, blocks_in(g) * P)]\
                .rearrange("d (p b) -> d b p", b=blocks_in(g))

        def rows_of(table, g):
            return table[bass.ds(first_block(g) * P, blocks_in(g) * P), :].rearrange("(p b) d -> p b d", b=blocks_in(g))

        parts, first_part = [], []
        for g in range(NG):
            first_part.append(len(parts))
            if g != 1:
                parts.append((0, max(g - 1, 0)))
            if 1 <= g < max(NG - 1, 2):
                parts.append((1, g - 1))
        first_part.append(len(parts))
        parts.append((0, NG - 1))
        early = len(parts)
        parts += [(1, g) for g in range(NG) if (1, g) not in parts]

        def parts_during(g):
            return range(first_part[g], first_part[g + 1])

        def part_by_act(u, q):
            return q >= 2 or (parts[u][0] == 1 and u < early)

        def stored_of(s, n):
            return sum(32 if parts[u][1] == NG - 1 else 16 for u in range(s, n, PQ))

        def tables_stored(eng, n):
            if n > early:
                eng.wait_ge(tail_stored, 16)
            for s in range(PQ):
                eng.wait_ge(pq_stored[s], stored_of(s, n))

        def rows_count(layer, i, s):
            short = layer + (isinstance(i, int) and i == HALF - 1) if s else 0
            return i * (16 * EIGHT) + ((layer * HALF + 1) * 16 * EIGHT - 16 * spare * short)

        def of_both(a, g):
            return a[:, :].rearrange("p (h b) -> p h b", h=2)[:, :, 0:blocks_in(g)]

        def any_stray(eng):
            eng.wait_ge(flag_ready, 1)
            return eng.value_load(flag[0:1, 0:1], min_val=0, max_val=2 * NT * P) > 0

        block = ctx.enter_context(nc.Block())

        @block.sync
        def _(sp):
            sp.dma_start(taken(x_sb, 0), rows_of(x, 0)).then_inc(x_in[0], 16)
            sp.dma_start(w_nodes[:, :], W_nodes).then_inc(w_nodes_in, 16)
            for g in range(1, NG + 1):
                sp.dma_start(taken(x_sb, g), rows_of(x, g)).then_inc(x_in[min(g, NG - 1)], 16)
            for to, of in (*((w_mixed[s][0:DE, b, :], W_edge) for s in range(2) for b in range(2)),
                           (w_gcn[1][:, :], W1), (w_gcn[2][:, :], W2), (b_gcn[1][:, :], b1.partition_broadcast(P)), (b_gcn[2][:, :], b2.partition_broadcast(P))):
                sp.dma_start(to, of).then_inc(weights_in, 16)
            for to, of in ((base_b[:, :], window_base.partition_broadcast(P)), (dst_i[:, :, :], dst_cols),
                           (ew_sb[:, :, :], ew_cols)):
                sp.dma_start(to, of).then_inc(index_in, 16)

            def load_idx(k, s):
                sp.dma_start(idx[s][:, :], src_tiles[bass.ds(k, 1), :, :].rearrange("a p j -> (a p) j"))\
                    .then_inc(idx_in[s], 16)

            def load_edges(k, s):
                sp.dma_start(dstw[s][:, :], dst_rows[bass.ds(k, 1), :].rearrange("a e -> (a e)").partition_broadcast(WIN))\
                    .then_inc(dstw_in[s], 16)
                sp.dma_start(edge_sb[s][:, :], edge_T[:, bass.ds(k * CE, CE)]).then_inc(edge_in[s], 16)

            def load_windows(k, s):
                bases = [sp.value_load(base_b[0:1, bass.ds(k * 2 + b, 1)], min_val=0, max_val=NPAD - 1) for b in range(2)]
                if not is_at_least(k, 2):
                    tables_stored(sp, 2 * NG)
                for b in range(2):
                    sp.dma_start(w_mixed[s][DE:P, b, :], table_dst[bass.ds(bases[b], WIN), :]).then_inc(window_in[s], 16)

            sp.wait_ge(zeros_made, 1)
            sp.dma_start(table_dst[NPAD:NPAD + P, :], sums[0][:, 0:2 * D]).then_inc(tail_stored, 16)
            for u, (which, g) in enumerate(parts):
                for q in range(4):
                    sp.wait_ge(copied[q], u + 1)
                for part in (g,) if g < NG - 1 else (NG - 1, NG):
                    at = (first_block(part) - g * GROUP)
                    sp.dma_start(rows_of((table_src, table_dst)[which], part), pq[u % PQ][:, at:at + blocks_in(part), :])\
                        .then_inc(pq_stored[u % PQ], 16)
                if u == early - 1:
                    for s in range(2):
                        load_idx(s, s)
                        load_edges(s, s)
            sp.wait_ge(index_in, 16 * N_INDEX)

            def store_rows(layer, g, F):
                sp.wait_ge(F.rows_made, F.count(layer, g))
                n = blocks_in(g)
                if layer < 2:
                    sp.dma_start(rows_of(tables[layer + 1], g), new_rows[:, 0:n, :]).then_inc(F.stored[layer], 16)
                elif isinstance(g, int) and g == NG:
                    start = first_block(g) * P
                    full = (NODES - start) // n
                    sp.dma_start(out[start:start + full * n, :].rearrange("(p b) d -> p b d", b=n), new_rows[0:full, 0:n, :])\
                        .then_inc(F.stored[layer], 16)
                    if OVER:
                        sp.dma_start(out[NODES - OVER:NODES, :].unsqueeze(0), new_rows[full:full + 1, 0:OVER, :])\
                            .then_inc(F.stored[layer], 16)
                else:
                    sp.dma_start(rows_of(out, g), new_rows[:, 0:n, :]).then_inc(F.stored[layer], 16)

            def free_rows(layer, g, F):
                sp.wait_ge(F.stored[layer], g * 16 + 16)
                sp.sem_inc(F.rows_free, 1)

            for F in (first_take, retake):
                sp.sem_inc(F.rows_free, 1)
            for layer in range(3):
                for what, i in schedule(sp, layer):
                    if what == "e" and not is_last(i) or what == "f" and is_last(i):
                        store_rows(layer, i, first_take)
                    if what == "f":
                        free_rows(layer, i, first_take)
                    if what == "chunk":
                        i, s = i
                        k = i * 2 + s
                        if is_at_least(i, 1):
                            sp.wait_ge(rows_in[s], rows_count(layer, i - 1, s))
                        if layer or is_at_least(i, 1):
                            load_idx(k, s)
                        if layer == 0:
                            if is_at_least(i, 1):
                                sp.wait_ge(z_ready, k * 4 - 4)
                                load_edges(k, s)
                            load_windows(k, s)
                if layer == 0:
                    store_rows(layer, NG - 1, first_take)
                    free_rows(layer, NG - 1, first_take)
                with sp.If(any_stray(sp)):
                    with sp.Fori(0, C) as c:
                        with sp.Fori(0, EIGHT) as j:
                            t = c * EIGHT + j
                            sp.wait_ge(f_next, t + (layer * (NT + 1) + 1))
                            sp.dma_start(idx[0][:, 0:1], src_tiles[bass.ds(c, 1), :, bass.ds(j, 1)]
                                         .rearrange("a p j -> (a p) j"), allow_slow_non_contiguous=True).then_inc(f_in, 16)
                            if layer == 0:
                                sp.dma_start(idx[1][:, 0:1], dst_tiles[bass.ds(c, 1), :, bass.ds(j, 1)]
                                             .rearrange("a p j -> (a p) j"), allow_slow_non_contiguous=True).then_inc(f_in, 16)
                                sp.dma_start(edge_sb[0][:, 0:P], edge_T[:, bass.ds(t * P, P)]).then_inc(f_in, 16)
                    with sp.Fori(0, NG - 1) as g:
                        store_rows(layer, g, retake)
                        free_rows(layer, g, retake)
                    store_rows(layer, NG - 1, retake)
                    free_rows(layer, NG - 1, retake)
                    sp.wait_ge(retaken, layer + 1)
                store_rows(layer, NG, first_take)
                if layer < 2:
                    free_rows(layer, NG, first_take)
            sp.wait_ge(first_take.stored[2], 16 * (NG + (2 if OVER else 1)))

        @block.gpsimd
        def _(pool):
            pool.iota(iota_i[:, :], pattern=[[1, P]], base=0, channel_multiplier=0).then_inc(ints_made, 1)
            pool.iota(part_i[:, :], pattern=[[0, 1]], base=0, channel_multiplier=1).then_inc(ints_made, 1)
            pool.memset(hT[:, 0:GROUP, :], 1.0).then_inc(ones_made, 1)
            pool.memset(first_node[:, 0:AHEAD], 0).then_inc(first_node_made, 1)
            pool.iota(first_node[:, AHEAD:].rearrange("p (g c) -> p g c", g=NG), pattern=[[GP, NG], [0, 2 * PAIRS]],
                      base=0, channel_multiplier=0).then_inc(first_node_made, 1)
            pool.wait_ge(first_node_made, 2)
            pool.iota(first_node[:, C - 2 - BEHIND:C], pattern=[[0, 2 + BEHIND]], base=first_block(NG) * P,
                      channel_multiplier=0).then_inc(first_node_made, 1)
            pool.iota(ident_i[:, :], pattern=[[1, P]], base=0, channel_multiplier=-1).then_inc(ints_made, 1)

            pool.memset(hT[:, GROUP:, :], 1.0).then_inc(ones_made, 1)
            pool.memset(sums[1][:, NPAD:], 0.0)
            pool.memset(sums[0][:, :], 0.0).then_inc(zeros_made, 1)

            def gather(to, table, index):
                return pool.indirect_dma_start(out=to, out_offset=None, in_=table,
                                               in_offset=bass.IndirectOffsetOnAxis(ap=index, axis=0))

            for g in range(NG):
                pool.wait_ge(h_made, g + 1)
                pool.tensor_tensor(blocks(xh, g), blocks(x_sb, g), new_rows[:, :, :], ALU.add).then_inc(xh_made, 1)

            for layer in range(3):
                table = table_src if layer == 0 else tables[layer]
                if layer == 0:
                    tables_stored(pool, early)
                else:
                    pool.wait_ge(first_take.stored[layer - 1], 16 * (NG + 1))

                def gather_pair(i):
                    for s in range(2):
                        k = i * 2 + s
                        tiles = EIGHT - spare if isinstance(i, int) and k == C - 1 else EIGHT
                        pool.wait_ge(idx_in[s], i * 16 + 16 * (layer * HALF + 1))
                        if is_at_least(i, 1):
                            if layer == 0:
                                pool.wait_ge(z_added, k * 4 - 4)
                            else:
                                pool.wait_ge(window_done, k + (layer * C - 1))
                        pool.sem_inc(gathers_let, 1)
                        to = rows[s] if layer == 0 else rows1[s]
                        for j in range(tiles):
                            gather(to[:, j, :], table, idx[s][:, j:j + 1]).then_inc(rows_in[s], 16)

                for i in range(2):
                    gather_pair(i)
                with pool.Fori(2, HALF - 1) as i:
                    gather_pair(i)
                gather_pair(HALF - 1)
                with pool.If(any_stray(pool)):
                    with pool.Fori(0, NT) as t:
                        if layer == 0:
                            pool.wait_ge(f_in, t * 48 + 48)
                            pool.sem_inc(gathers_let, 1)
                            gather(rows[0][:, 0, :], table_src, idx[0][:, 0:1]).then_inc(f_rows, 16)
                            gather(rows[1][:, 0, :], table_dst, idx[1][:, 0:1]).then_inc(f_rows, 16)
                        else:
                            pool.wait_ge(f_in, t * 16 + (48 * NT + 16 * (layer - 1) * NT + 16))
                            pool.sem_inc(gathers_let, 1)
                            gather(rows1[0][:, 0, :], table, idx[0][:, 0:1]).then_inc(f_rows, 16)
                    pool.wait_ge(retaken, layer + 1)
                    pool.wait_ge(retake.stored[layer], 16 * NG)

        @block.scalar
        def _(act):
            def p_square(g):
                act.wait_ge(p_xc, g + 1)
                act.activation(blocks(xh, g), p_xc_t[g % 2][:, :, :], ACT.Square).then_inc(p_sq, 1)

            def p_copy(u):
                if u >= PQ:
                    act.wait_ge(pq_stored[u % PQ], stored_of(u % PQ, u))
                for q in range(4):
                    if part_by_act(u, q):
                        n = 2 if q < 3 else 1
                        act.wait_ge(node_prod, 4 * u + q + 1)
                        act.activation(pq[u % PQ][:, 2 * q:2 * q + n, :].rearrange("p b n -> p (b n)"),
                                       ps_z[:, q, 0:n * 2 * D], ACT.Copy).then_inc(copied[q], 1)

            def p_roots(g):
                act.wait_ge(p_root_in, g + 1)
                act.activation(root[:, 0:GROUP], root_in[:, 0:GROUP], ACT.Sqrt).then_inc(p_root, 1)

            act.preload_act_table_set("sqrt_and_others")
            for g in range(2):
                p_square(g)
            p_roots(0)
            for g in range(NG):
                act.wait_ge(ones_made, 1 if g == 0 else 2)
                act.wait_ge(h_turned, g + 1)
                act.activation(hT[0:D, g * GROUP:(g + 1) * GROUP, :], ps_t[0:D, 0:GROUP, :], ACT.Copy).then_inc(hT_made, 1)
                if g + 2 < NG:
                    p_square(g + 2)
                if g + 1 < NG:
                    p_roots(g + 1)
                for u in parts_during(g):
                    p_copy(u)
            for u in range(early - 1, 2 * NG):
                p_copy(u)

            def logs(k, s):
                act.wait_ge(z_added, k * 4 + 4)
                if is_at_least(k, 2):
                    act.wait_ge(plus_made, k - 1)
                act.activation(az[s][:, :, :, :], z[s][:, :, :, :], ACT.Abs).then_inc(absd, 1)
                act.wait_ge(absd, k + 1)
                act.activation(az[s][:, :, :, :], az[s][:, :, :, :], ACT.Exp, scale=-1.0).then_inc(expd, 1)
                act.wait_ge(expd, k + 1)
                act.activation(az[s][:, :, :, :], az[s][:, :, :, :], ACT.Ln, bias=1.0).then_inc(logd, 1)

            def gates(k, s):
                act.wait_ge(gate_arg, k + 1)
                act.activation(gp[s][:, :, 0, :], gp[s][:, :, 0, :], ACT.Exp).then_inc(gate_made, 1)

            def step(k, s):
                if is_chunk(k - 1):
                    logs(k - 1, 1 - s)
                if is_chunk(k - 2):
                    gates(k - 2, s)

            act.preload_act_table_set("natural_log_exp_and_others")
            def stage(layer, g, F):
                n = F.count(layer, g)
                act.wait_ge(F.turned, n)
                behind = 1 if layer else BEHIND
                if F is retake or isinstance(g, int) and g == NG:
                    act.wait_ge(window_added, (layer + 1) * 2 * C)
                elif is_last(g):
                    act.wait_ge(window_added, 2 * (layer * C + C - 2 - behind))
                else:
                    act.wait_ge(window_added, g * (4 * PAIRS) + 2 * (layer * C + 2 * (PAIRS + LEAD) - behind))
                width = D if layer else DX
                act.activation(staged_T[0:width, 0:blocks_in(g) * P].rearrange("d (b p) -> d b p", p=P),
                               sums_of(layer, g, width), ACT.Copy).then_inc(F.staged, 1)

            def squares(g, F):
                act.wait_ge(F.xc, F.count(0, g))
                n = blocks_in(g)
                act.activation(sq[:, 0:n, :], xc[:, 0:n, :], ACT.Square).then_inc(F.sq, 1)

            def roots(g, F):
                act.wait_ge(F.root_in, F.count(0, g) * 2)
                act.activation(of_both(root, g), of_both(root_in, g), ACT.Sqrt).then_inc(F.root, 1)

            def begin_sums(layer, g, F):
                act.wait_ge(F.rows_turned, F.count(layer, g) + 1)
                act.activation(sums_of(layer + 1, g, D), ps_t[0:D, 0:blocks_in(g), :], ACT.Copy)\
                    .then_inc(F.t_free, 1)

            def take(layer, g, F, what):
                last = F is first_take and isinstance(g, int) and g >= NG - 1
                if what == "a":
                    stage(layer, g, F)
                if what == "b" and layer == 0:
                    squares(g, F)
                if what == "c" and layer == 0:
                    roots(g, F)
                    if not last:
                        act.preload_act_table_set("natural_log_exp_and_others")
                if what == "e" and layer < 2:
                    begin_sums(layer, g, F)

            def retake_all(layer):
                v = first_take.count(layer, NG)
                act.wait_ge(first_take.turned, v)
                act.wait_ge(strays_added, layer + 1)
                with act.Fori(0, NG - 1) as g:
                    for what in "abcde":
                        take(layer, g, retake, what)
                for what in "abcde":
                    take(layer, NG - 1, retake, what)
                act.wait_ge(retaken, layer + 1)

            for F in (first_take, retake):
                act.sem_inc(F.t_free, 1)
            for what, i in schedule(act, 0):
                if what == "chunk":
                    step(i[0] * 2 + i[1], i[1])
                else:
                    take(0, i, first_take, what)
            for k in range(C, C + 2):
                step(k, k % 2)
            for what in "cde":
                take(0, NG - 1, first_take, what)

            with act.If(any_stray(act)):
                act.preload_act_table_set("natural_log_exp_and_others")
                with act.Fori(0, NT) as t:
                    act.wait_ge(f_z2, t + 1)
                    act.activation(az[0][:, 0, :, :], z[0][:, 0, :, :], ACT.Abs).then_inc(f_abs, 1)
                    act.wait_ge(f_abs, t + 1)
                    act.activation(az[0][:, 0, :, :], az[0][:, 0, :, :], ACT.Exp, scale=-1.0).then_inc(f_exp, 1)
                    act.wait_ge(f_exp, t + 1)
                    act.activation(az[0][:, 0, :, :], az[0][:, 0, :, :], ACT.Ln, bias=1.0).then_inc(f_log, 1)
                    act.wait_ge(f_arg, t + 1)
                    act.activation(az[0][:, 0, 0, :], az[0][:, 0, 0, :], ACT.Exp).then_inc(f_gate, 1)
                retake_all(0)
            act.preload_act_table_set("sqrt_and_others")
            for what in "abcde":
                take(0, NG, first_take, what)

            for layer in (1, 2):
                with act.Fori(0, NG - 1) as g:
                    for what in "abcde":
                        take(layer, g, first_take, what)
                for what in "abcde":
                    take(layer, NG - 1, first_take, what)
                with act.If(any_stray(act)):
                    retake_all(layer)
                for what in "abcde":
                    take(layer, NG, first_take, what)

        @block.tensor
        def _(pe):
            pe.wait_ge(consts_made, 3)
            pe.wait_ge(ident_made, 1)
            pe.wait_ge(w_nodes_in, 16)
            def node_products(u):
                which, g = parts[u]
                pe.wait_ge(hT_made, g + 1)
                for q in range(4):
                    if u >= 1:
                        pe.wait_ge(copied[q], u)
                    for j in range(2 * q, min(2 * q + 2, GROUP)):
                        last = pe.matmul(ps_z[:, q, (j % 2) * 2 * D:(j % 2 + 1) * 2 * D], hT[:, g * GROUP + j, :],
                                         w_nodes[:, which * 2 * D:(which + 1) * 2 * D], start=True, stop=True)
                    last.then_inc(node_prod, 1)

            for g in range(NG):
                pe.wait_ge(h_made, g + 1)
                if g >= 1:
                    pe.wait_ge(hT_made, g)
                for j in range(GROUP):
                    last = pe.transpose(ps_t[0:D, j, :], new_rows[:, j, :], ident[:, :])
                last.then_inc(h_turned, 1)
                for u in parts_during(g):
                    node_products(u)
            for u in range(early - 1, 2 * NG):
                node_products(u)
            pe.wait_ge(stray_counted, 2)
            pe.matmul(ps_w[0][0:1, 0:1], ones[:, :], strays[:, 0:1], start=True, stop=False)
            pe.matmul(ps_w[0][0:1, 0:1], ones[:, :], strays[:, 1:2], start=False, stop=True).then_inc(stray_summed, 1)

            def products(k, s, i):
                pe.wait_ge(edge_in[s], i * 16 + 16)
                pe.wait_ge(window_in[s], i * 32 + 32)
                pe.wait_ge(hotT_made, k + 1)
                for q in range(4):
                    if not is_at_least(k, 1):
                        pe.wait_ge(copied[q], 2 * NG)
                    else:
                        pe.wait_ge(z_added, k * 4 + (q - 3))
                    for j in (2 * q, 2 * q + 1):
                        to = ps_z[:, q, (j % 2) * 2 * D:(j % 2 + 1) * 2 * D]
                        last = pe.matmul(to, mixed[s][:, j * P:(j + 1) * P], w_mixed[s][:, j // FOUR, :], start=True, stop=True)
                    last.then_inc(z_ready, 1)

            def window(K, s, rows_of, width):
                pe.wait_ge(hot_made, K + 1)
                if is_at_least(K, 2):
                    pe.wait_ge(window_added, K * 2 - 2)
                for j in range(EIGHT):
                    b = j // FOUR
                    last = pe.matmul(ps_w[s][0:width, b * WIN:(b + 1) * WIN], rows_of[:, j, :], hot[s][:, j, :],
                                     start=(j % FOUR == 0), stop=(j % FOUR == FOUR - 1))
                last.then_inc(window_done, 1)

            def first_layer_step(k, s, i):
                if is_chunk(k):
                    products(k, s, i)
                if is_chunk(k - 3):
                    pe.wait_ge(msg_made, k * 2 - 4)
                    window(k - 3, 1 - s, msg[1 - s], DX)

            def stray_windows(layer, t):
                with pe.Fori(0, NB) as w:
                    n = t * NB + w
                    pe.wait_ge(f_hot, n + (layer * NT * NB + 1))
                    pe.matmul(ps_w[0][0:DX, 0:P], msg_one[:, :], hot_one, start=True, stop=True).then_inc(f_sum, 1)

            def turn_sums(layer, g, F):
                n = F.count(layer, g)
                pe.wait_ge(F.staged, n)
                pe.wait_ge(F.t_free, n)
                for j in range(blocks_in(g)):
                    if layer == 0:
                        last = pe.transpose(ps_t[:, j, 0:DX], staged_T[0:DX, j * P:(j + 1) * P], ident[0:DX, 0:DX])
                    else:
                        last = pe.matmul(ps_t[:, j, 0:D], staged_T[0:D, j * P:(j + 1) * P], w_gcn[layer][:, :],
                                         start=True, stop=True)
                last.then_inc(F.turned, 1)

            def turn_rows(layer, g, F):
                pe.wait_ge(F.rows_made, F.count(layer, g))
                for j in range(blocks_in(g)):
                    last = pe.transpose(ps_t[0:D, j, :], new_rows[:, j, :], ident[:, :])
                last.then_inc(F.rows_turned, 1)

            def take(layer, g, F, what):
                if what == "a":
                    turn_sums(layer, g, F)
                if what == "e" and layer < 2:
                    turn_rows(layer, g, F)

            def retake_all(layer):
                pe.wait_ge(first_take.t_free, first_take.count(layer, NG))
                with pe.Fori(0, NG - 1) as g:
                    for what in "abcde":
                        take(layer, g, retake, what)
                for what in "abcde":
                    take(layer, NG - 1, retake, what)
                pe.wait_ge(retaken, layer + 1)

            for F in (first_take, retake):
                pe.sem_inc(F.turned, 1)
                pe.sem_inc(F.rows_turned, 1)
            pe.wait_ge(weights_in, 16 * N_WEIGHTS)
            pe.wait_ge(flag_ready, 1)
            for what, i in schedule(pe, 0):
                if what == "chunk":
                    first_layer_step(i[0] * 2 + i[1], i[1], i[0])
                else:
                    take(0, i, first_take, what)
            for k in range(C, C + 3):
                first_layer_step(k, k % 2, None)
            take(0, NG - 1, first_take, "e")
            with pe.If(any_stray(pe)):
                with pe.Fori(0, NT) as t:
                    pe.wait_ge(f_in, t * 48 + 48)
                    pe.matmul(ps_z[:, 0, 0:2 * D], edge_sb[0][:, 0:P], w_mixed[0][0:DE, 0, :], start=True, stop=True)\
                        .then_inc(f_z, 1)
                    stray_windows(0, t)
                retake_all(0)
            for what in "abcde":
                take(0, NG, first_take, what)

            for layer in (1, 2):
                for what, i in schedule(pe, layer):
                    if what == "chunk":
                        i, s = i
                        pe.wait_ge(rows_in[s], rows_count(layer, i, s))
                        window(i * 2 + (layer * C + s), s, rows1[s], D)
                    else:
                        take(layer, i, first_take, what)
                with pe.If(any_stray(pe)):
                    with pe.Fori(0, NT) as t:
                        stray_windows(layer, t)
                    retake_all(layer)
                for what in "abcde":
                    take(layer, NG, first_take, what)

        @block.vector
        def _(dve):
            TT, TS = dve.tensor_tensor, dve.tensor_scalar
            dve.memset(ones[:, :], 1.0).then_inc(consts_made, 1)
            for s in range(2):
                dve.memset(msg[s][:, :, D:D + 1], 1.0)
            dve.memset(msg_one[:, :], 0.0)
            dve.wait_ge(ints_made, 3)
            dve.tensor_copy(iota_f[:, :], iota_i[:, :]).then_inc(consts_made, 1)
            dve.tensor_copy(part_f[:, :], part_i[:, :]).then_inc(consts_made, 1)
            TS(ident[:, :], ident_i[:, :], 0.0, None, ALU.is_equal).then_inc(ident_made, 1)
            dve.wait_ge(consts_made, 3)

            def p_center(g):
                dve.wait_ge(x_in[g], 16 if g < NG - 1 else 32)
                dve.reduce_sum(total[:, :], blocks(x_sb, g), X).then_inc(p_total, 1)
                dve.wait_ge(p_total, g + 1)
                TS(nmean[:, :], total[:, :], -1.0 / D, None, ALU.mult).then_inc(p_nmean, 1)
                dve.wait_ge(p_nmean, g + 1)
                TT(p_xc_t[g % 2][:, :, :], blocks(x_sb, g), along(nmean[:, :], D), ALU.add).then_inc(p_xc, 1)
                dve.wait_ge(p_xc, g + 1)

            def p_variance(g):
                dve.wait_ge(p_sq, g + 1)
                dve.reduce_sum(var[:, :], blocks(xh, g), X).then_inc(p_var, 1)
                dve.wait_ge(p_var, g + 1)
                TS(root_in[:, 0:GROUP], var[:, :], 1.0 / D, EPS, ALU.mult, ALU.add).then_inc(p_root_in, 1)

            def p_rows(g):
                dve.wait_ge(p_root, g + 1)
                dve.reciprocal(rroot[:, 0:GROUP], root[:, 0:GROUP]).then_inc(p_rroot, 1)
                dve.wait_ge(p_rroot, g + 1)
                if g >= 1:
                    dve.wait_ge(h_turned, g)
                    dve.wait_ge(xh_made, g)
                relu_times(new_rows[:, :, :], p_xc_t[g % 2][:, :, :], rroot[:, 0:GROUP]).then_inc(h_made, 1)
                dve.wait_ge(h_made, g + 1)

            def p_copy(u):
                if part_by_act(u, 0):
                    return
                if u >= PQ:
                    dve.wait_ge(pq_stored[u % PQ], stored_of(u % PQ, u))
                for q in range(2):
                    dve.wait_ge(node_prod, 4 * u + q + 1)
                    dve.tensor_copy(pq[u % PQ][:, 2 * q:2 * q + 2, :].rearrange("p b n -> p (b n)"), ps_z[:, q, 0:4 * D])\
                        .then_inc(copied[q], 1)

            def relu_times(out, a, scale):
                return dve.scalar_tensor_tensor(out=out, in0=a, scalar=0.0, in1=along(scale, D), op0=ALU.max, op1=ALU.mult)

            def count_strays():
                dve.wait_ge(index_in, 16 * N_INDEX)
                TS(window_node[:, :], base_b[:, :], part_f[:, :], float(-DE), ALU.add, ALU.add)
                TT(halves(dst_rel), halves(dst_i), along(base_b[:, :], FOUR), ALU.subtract).then_inc(rel_made, 1)
                yield
                dve.wait_ge(first_node_made, 3)
                TT(late[:, :, :], dst_i[:, :, :], along(first_node[:, 0:C], EIGHT), ALU.is_lt).then_inc(late_made, 1)
                yield
                dve.wait_ge(rel_made, 1)
                TS(stray[:, :, :], dst_rel[:, :, :], float(WIN), None, ALU.is_ge).then_inc(inside_made, 1)
                yield
                dve.wait_ge(inside_made, 1)
                dve.scalar_tensor_tensor(out=stray[:, :, :], in0=dst_rel[:, :, :], scalar=0.0, in1=stray[:, :, :],
                                         op0=ALU.is_lt, op1=ALU.add).then_inc(stray_made, 1)
                yield
                dve.wait_ge(late_made, 1)
                dve.reduce_sum(strays[:, 1:2], late[:, :, :].rearrange("p c j -> p (c j)"), X).then_inc(stray_counted, 1)
                yield
                dve.wait_ge(stray_made, 1)
                dve.reduce_sum(strays[:, 0:1], stray[:, :, :].rearrange("p c j -> p (c j)"), X).then_inc(stray_counted, 1)
                yield

            for g in range(2):
                p_center(g)
            p_variance(0)
            for g in range(NG):
                p_rows(g)
                if g + 2 < NG:
                    p_center(g + 2)
                if g + 1 < NG:
                    p_variance(g + 1)
                for u in parts_during(g):
                    p_copy(u)
            counting = count_strays()
            for u in range(early - 1, 2 * NG):
                p_copy(u)
                next(counting, None)
                next(counting, None)
            for _ in counting:
                pass
            dve.wait_ge(stray_summed, 1)
            dve.tensor_copy(flag[:, :], ps_w[0][0:1, 0:1]).then_inc(flag_ready, 1)

            def targets_hot(k, s, i):
                dve.wait_ge(dstw_in[s], i * 16 + 16)
                for b in range(2):
                    half = slice(b * FOUR * P, (b + 1) * FOUR * P)
                    made = TS(hotT[s][:, half], dstw[s][:, half], window_node[DE:P, bass.ds(k * 2 + b, 1)], None, ALU.is_equal)
                made.then_inc(hotT_made, 1)

            def add_sources(k, s, i):
                if not is_at_least(k, 1):
                    dve.wait_ge(xh_made, NG)
                    dve.wait_ge(h_turned, NG)
                    tables_stored(dve, 2 * NG)
                dve.wait_ge(rows_in[s], rows_count(0, i, s))
                if is_at_least(k, 2):
                    dve.wait_ge(plus_made, k - 1)
                for q in range(4):
                    dve.wait_ge(z_ready, k * 4 + (q + 1))
                    TT(z[s][:, 2 * q:2 * q + 2, :, :].rearrange("p a b d -> p (a b d)"), ps_z[:, q, 0:4 * D],
                       rows[s][:, 2 * q:2 * q + 2, :].rearrange("p a d -> p (a d)"), ALU.add).then_inc(z_added, 1)

            def sum_args(k, s):
                dve.wait_ge(logd, k + 1)
                if is_at_least(k, 2):
                    dve.wait_ge(msg_made, k * 2 - 2)
                dve.scalar_tensor_tensor(out=gp[s][:, :, 0, :], in0=z[s][:, :, 0, :], scalar=0.0, in1=az[s][:, :, 0, :],
                                         op0=ALU.min, op1=ALU.subtract).then_inc(gate_arg, 1)
                dve.scalar_tensor_tensor(out=gp[s][:, :, 1, :], in0=z[s][:, :, 1, :], scalar=0.0, in1=az[s][:, :, 1, :],
                                         op0=ALU.max, op1=ALU.add).then_inc(plus_made, 1)

            def messages(k, s):
                dve.wait_ge(gate_made, k + 1)
                dve.wait_ge(plus_made, k + 1)
                if is_at_least(k, 2):
                    dve.wait_ge(window_done, k - 1)
                TT(msg[s][:, :, 0:D], gp[s][:, :, 0, :], gp[s][:, :, 1, :], ALU.mult).then_inc(msg_made, 1)
                dve.tensor_copy(msg[s][:, :, D + 1:DX].rearrange("p j a -> p (j a)"),
                                ew_sb[:, bass.ds(k, 1), :].rearrange("p a j -> p (a j)")).then_inc(msg_made, 1)

            def targets(k, s, K, weighted):
                rel_k = dst_rel[:, bass.ds(k, 1), :].rearrange("p a j -> p (a j)")
                to = hoti[s] if weighted else hot[s]
                if weighted:
                    dve.wait_ge(hot_made, K - 1)
                elif is_at_least(K, 2):
                    dve.wait_ge(window_done, K - 1)
                made = TT(to[:, :, :], across(iota_f[:, 0:WIN], EIGHT), along(rel_k, WIN), ALU.is_equal)
                if not weighted:
                    made.then_inc(hot_made, 1)
                    return
                made.then_inc(equal_made, 1)
                dve.wait_ge(equal_made, K - C + 1)
                TT(hot[s][:, :, :], hoti[s][:, :, :], along(ew_sb[:, bass.ds(k, 1), :].rearrange("p a j -> p (a j)"), WIN),
                   ALU.mult).then_inc(hot_made, 1)

            def add_window(k, s, K, width, layer=0, staged=None):
                at = []
                for b in range(2):
                    base = dve.value_load(base_b[0:1, bass.ds(k * 2 + b, 1)], min_val=0, max_val=NPAD - 1)
                    at.append(sums[layer % 2][0:width, bass.ds(base, WIN)])
                dve.wait_ge(window_done, K + 1)
                if is_at_least(K, 1):
                    dve.wait_ge(window_added, K * 2)
                if staged is not None:
                    dve.wait_ge(first_take.staged, first_take.count(layer, staged))
                for b in range(2):
                    if b:
                        dve.wait_ge(window_added, K * 2 + 1)
                    TT(at[b], at[b], ps_w[s][0:width, b * WIN:(b + 1) * WIN], ALU.add).then_inc(window_added, 1)

            def first_layer_step(k, s, i, staged=None):
                if is_chunk(k):
                    targets_hot(k, s, i)
                if is_chunk(k - 1):
                    add_sources(k - 1, 1 - s, i if s else i - 1)
                if is_chunk(k - 2):
                    sum_args(k - 2, s)
                if is_chunk(k - 4):
                    add_window(k - 4, s, k - 4, DX, 0, staged)
                if is_chunk(k - 3):
                    targets(k - 3, 1 - s, k - 3, False)
                    messages(k - 3, 1 - s)

            def strays_of(layer):
                dve.drain().then_inc(f_next, 1)
                with dve.Fori(0, C) as c:
                    with dve.Fori(0, EIGHT) as j:
                        t = c * EIGHT + j
                        T = t + layer * NT
                        stray_t = stray[:, bass.ds(c, 1), bass.ds(j, 1)].rearrange("p a b -> p (a b)")
                        ew_t = ew_sb[:, bass.ds(c, 1), bass.ds(j, 1)].rearrange("p a b -> p (a b)")
                        dst_t = dst_i[:, bass.ds(c, 1), bass.ds(j, 1)].rearrange("p a b -> p (a b)")
                        if layer == 0:
                            zt, at = z[0][:, 0, :, :], az[0][:, 0, :, :]
                            flat = zt.rearrange("p b d -> p (b d)")
                            dve.wait_ge(f_rows, t * 32 + 32)
                            dve.wait_ge(f_z, t + 1)
                            TT(flat, ps_z[:, 0, 0:2 * D], rows[0][:, 0, :], ALU.add).then_inc(f_z1, 1)
                            dve.wait_ge(f_z1, t + 1)
                            TT(flat, flat, rows[1][:, 0, :], ALU.add).then_inc(f_z2, 1)
                            dve.wait_ge(f_z2, t + 1)
                            dve.wait_ge(f_log, t + 1)
                            dve.scalar_tensor_tensor(out=at[:, 0, :], in0=zt[:, 0, :], scalar=0.0, in1=at[:, 0, :],
                                                     op0=ALU.min, op1=ALU.subtract).then_inc(f_arg, 1)
                            dve.scalar_tensor_tensor(out=at[:, 1, :], in0=zt[:, 1, :], scalar=0.0, in1=at[:, 1, :],
                                                     op0=ALU.max, op1=ALU.add).then_inc(f_plus, 1)
                            dve.tensor_copy(msg[0][:, 0, D + 1:DX], ew_t).then_inc(f_prod, 1)
                            dve.wait_ge(f_plus, t + 1)
                            dve.wait_ge(f_gate, t + 1)
                            TT(msg[0][:, 0, 0:D], at[:, 0, :], at[:, 1, :], ALU.mult).then_inc(f_prod, 1)
                            dve.wait_ge(f_prod, t * 2 + 2)
                            TS(msg_one[:, :], msg[0][:, 0, :], stray_t, None, ALU.mult).then_inc(f_msg, 1)
                        else:
                            dve.wait_ge(f_rows, t * 16 + (32 * NT + 16 * (layer - 1) * NT + 16))
                            TS(msg_one[:, 0:D], rows1[0][:, 0, :], stray_t, ew_t, ALU.mult, ALU.mult).then_inc(f_msg, 1)
                        dve.tensor_copy(rel[:, :], dst_t).then_inc(f_rel, 1)
                        with dve.Fori(0, NB) as w:
                            n = T * NB + w
                            dve.wait_ge(f_msg, T + 1)
                            dve.wait_ge(f_rel, n + T + 1)
                            TS(hot_one, iota_f[:, :], rel[:, :], None, ALU.is_equal).then_inc(f_hot, 1)
                            dve.wait_ge(f_hot, n + 1)
                            TS(rel[:, :], rel[:, :], float(-P), None, ALU.add).then_inc(f_rel, 1)
                            width = D if layer else DX
                            at_w = sums[layer % 2][0:width, bass.ds(w * P, P)]
                            dve.wait_ge(f_sum, n + 1)
                            TT(at_w, at_w, ps_w[0][0:width, 0:P], ALU.add).then_inc(f_acc, 1)
                            dve.wait_ge(f_acc, n + 1)
                        dve.drain().then_inc(f_next, 1)
                dve.drain().then_inc(strays_added, 1)

            def center(g, F):
                n, b = F.count(0, g), blocks_in(g)
                dve.wait_ge(F.turned, n + 1)
                TS(cnt[:, 0:b], ps_t[:, 0:b, D], 1.0, None, ALU.max).then_inc(F.cnt, 1)
                TS(dpos[:, 0:b], ps_t[:, 0:b, D + 1], 1.0, 0.0, ALU.add, ALU.is_gt).then_inc(F.dpos, 1)
                TS(of_both(root_in, g)[:, 1, :], ps_t[:, 0:b, D + 1], 1.0, 1e-30, ALU.add, ALU.max).then_inc(F.root_in, 1)
                dve.wait_ge(F.cnt, n)
                dve.reciprocal(rcnt[:, 0:b], cnt[:, 0:b]).then_inc(F.rcnt, 1)
                dve.wait_ge(F.rcnt, n)
                TT(sq[:, 0:b, :], ps_t[:, 0:b, 0:D], along(rcnt[:, 0:b], D), ALU.mult).then_inc(F.hnew, 1)
                dve.wait_ge(F.hnew, n)
                TT(taken(x_sb, g), sq[:, 0:b, :], taken(xh, g), ALU.add).then_inc(F.x1, 1)
                dve.wait_ge(F.x1, n)
                dve.sem_inc(sums_let, 1)
                dve.reduce_sum(total[:, 0:b], taken(x_sb, g), X).then_inc(F.total, 1)
                dve.wait_ge(F.total, n)
                TS(nmean[:, 0:b], total[:, 0:b], -1.0 / D, None, ALU.mult).then_inc(F.nmean, 1)
                dve.wait_ge(F.nmean, n)
                TT(xc[:, 0:b, :], taken(x_sb, g), along(nmean[:, 0:b], D), ALU.add).then_inc(F.xc, 1)

            def free_to_write(n, F):
                dve.wait_ge(F.rows_free, n)
                dve.wait_ge(F.rows_turned, n)

            def variance(g, F):
                n, b = F.count(0, g), blocks_in(g)
                dve.wait_ge(F.sq, n)
                dve.reduce_sum(var[:, 0:b], sq[:, 0:b, :], X).then_inc(F.var, 1)
                dve.wait_ge(F.var, n)
                TS(root_in[:, 0:b], var[:, 0:b], 1.0 / D, EPS, ALU.mult, ALU.add).then_inc(F.root_in, 1)

            def rows_first(g, F):
                n, b = F.count(0, g), blocks_in(g)
                dve.wait_ge(F.root, n)
                dve.reciprocal(of_both(rroot, g), of_both(root, g)).then_inc(F.rroot, 1)
                dve.wait_ge(F.rroot, n)
                dve.wait_ge(F.dpos, n)
                TT(columns(dinv, g), of_both(rroot, g)[:, 1, :], dpos[:, 0:b], ALU.mult).then_inc(F.dinv, 1)
                dve.wait_ge(F.dinv, n)
                TT(rd[:, 0:b], rroot[:, 0:b], columns(dinv, g), ALU.mult).then_inc(F.rd, 1)
                dve.wait_ge(F.rd, n)
                free_to_write(n, F)
                relu_times(new_rows[:, 0:b, :], xc[:, 0:b, :], rd[:, 0:b]).then_inc(F.rows_made, 1)

            def rows_gcn(layer, g, F):
                n, b = F.count(layer, g), blocks_in(g)
                m = n - F.per_layer
                dve.wait_ge(F.turned, n + 1)
                scaled = TT(xc[:, 0:b, :], ps_t[:, 0:b, 0:D], along(columns(dinv, g), D), ALU.mult)
                scaled.then_inc(F.scaled, 1)
                dve.wait_ge(F.scaled, m)
                if layer == 2:
                    dve.sem_inc(F.t_free, 1)
                TT(sq[:, 0:b, :], xc[:, 0:b, :], across(b_gcn[layer][:, :], b), ALU.add).then_inc(F.biased, 1)
                dve.wait_ge(F.biased, m)
                if layer == 1:
                    free_to_write(n, F)
                    relu_times(new_rows[:, 0:b, :], sq[:, 0:b, :], columns(dinv, g)).then_inc(F.rows_made, 1)
                else:
                    dve.wait_ge(F.rows_free, n)
                    dve.scalar_tensor_tensor(out=new_rows[:, 0:b, :], in0=sq[:, 0:b, :], scalar=0.0, in1=taken(x_sb, g),
                                             op0=ALU.max, op1=ALU.add).then_inc(F.rows_made, 1)

            def take(layer, g, F, what):
                if what == "b":
                    if layer == 0:
                        center(g, F)
                    else:
                        rows_gcn(layer, g, F)
                if what == "c" and layer == 0:
                    variance(g, F)
                if what == "d" and layer == 0:
                    rows_first(g, F)

            def retake_all(layer):
                v = first_take.count(layer, NG)
                dve.wait_ge(first_take.rows_free, v)
                dve.wait_ge(first_take.t_free, v)
                with dve.Fori(0, NG - 1) as g:
                    for what in "abcd":
                        take(layer, g, retake, what)
                for what in "abcd":
                    take(layer, NG - 1, retake, what)
                v = retake.count(layer, NG)
                dve.wait_ge(retake.rows_free, v)
                dve.wait_ge(retake.t_free, v)
                dve.drain().then_inc(retaken, 1)

            staged = None
            for what, i in schedule(dve, 0):
                if what == "chunk":
                    first_layer_step(i[0] * 2 + i[1], i[1], i[0], staged)
                    staged = None
                else:
                    take(0, i, first_take, what)
                    if what == "a":
                        staged = i
            first_layer_step(C, 0, C // 2)
            targets(C - 2, 0, C - 2, False)
            sum_args(C - 1, 1)
            messages(C - 2, 0)
            targets(C - 1, 1, C - 1, False)
            messages(C - 1, 1)
            add_window(C - 3, 1, C - 3, DX)
            for what in "cd":
                take(0, NG - 1, first_take, what)
            add_window(C - 2, 0, C - 2, DX)
            add_window(C - 1, 1, C - 1, DX)
            dve.wait_ge(window_added, 2 * C)
            with dve.If(any_stray(dve)):
                strays_of(0)
                retake_all(0)
            for what in "abcd":
                take(0, NG, first_take, what)

            for layer in (1, 2):
                dve.wait_ge(first_take.t_free, layer * (NG + 1) + 1)
                staged = None
                for what, i in schedule(dve, layer):
                    if what == "chunk":
                        i, s = i
                        k = i * 2 + s
                        targets(k, s, k + layer * C, True)
                        if is_chunk(k - 1):
                            add_window(k - 1, 1 - s, k + (layer * C - 1), D, layer, staged)
                            staged = None
                        continue
                    take(layer, i, first_take, what)
                    if what == "a":
                        staged = i
                add_window(C - 1, 1, (layer + 1) * C - 1, D, layer)
                dve.wait_ge(window_added, (layer + 1) * 2 * C)
                with dve.If(any_stray(dve)):
                    strays_of(layer)
                    retake_all(layer)
                take(layer, NG, first_take, "b")


def kernel(x, src, dst, edge_attr_64, edge_weight, L0_gnn_W_e, L0_gnn_b_e, L0_gnn_W_n, L0_gnn_b_n,
           L1_gnn_W1, L1_gnn_b1, L1_gnn_W2, L1_gnn_b2):
    import numpy as np
    import concourse.bacc as bacc
    from concourse.bass_utils import run_bass_kernel_spmd as run

    nodes, edges = x.shape[0], src.shape[0]
    node_pad = -nodes % (P * GROUP)
    tile_pad = -edges % (2 * P * EIGHT)
    chunks = (edges + tile_pad) // (P * EIGHT)
    x = np.pad(np.asarray(x), ((0, node_pad), (0, 0)))
    src = np.pad(np.asarray(src), (0, tile_pad)).reshape(chunks, EIGHT, P)
    dst = np.pad(np.asarray(dst), (0, tile_pad), constant_values=nodes).reshape(chunks, EIGHT, P)
    ew = np.pad(np.asarray(edge_weight), (0, tile_pad)).reshape(chunks, EIGHT, P)
    edge_T = np.pad(np.asarray(edge_attr_64), ((0, tile_pad), (0, 0))).T
    W_e, W_n = np.asarray(L0_gnn_W_e), np.asarray(L0_gnn_W_n)
    both = np.concatenate([W_e, W_n], axis=1)
    bias = np.concatenate([np.zeros_like(both[0]), np.asarray(L0_gnn_b_e), np.asarray(L0_gnn_b_n)])
    arrays = {
        "x": x, "src_tiles": src.transpose(0, 2, 1), 
        "dst_rows": dst.reshape(chunks, EIGHT * P), "dst_cols": dst.transpose(2, 0, 1), "dst_tiles": dst.transpose(0, 2, 1),
        "ew_cols": ew.transpose(2, 0, 1), "window_base": dst[:, ::FOUR, 0].reshape(-1), "edge_T": edge_T,
        "W_nodes": np.concatenate([np.concatenate([both[0:D], both[D:2 * D]], axis=1), bias[None]]), "W_edge": both[2 * D:],
        "W1": np.asarray(L1_gnn_W1), "b1": np.asarray(L1_gnn_b1), "W2": np.asarray(L1_gnn_W2), "b2": np.asarray(L1_gnn_b2),
    }
    nc = bacc.Bacc("TRN2", target_bir_lowering=False, num_devices=1)
    args, feeds = {}, {}
    for name, a in arrays.items():
        feeds[f"in_{name}"] = a = np.ascontiguousarray(a)
        args[name] = nc.dram_tensor(f"in_{name}", a.shape, mybir.dt.from_np(a.dtype), kind="ExternalInput").ap()
    args["out"] = nc.dram_tensor("out_0", (nodes, D), F32, kind="ExternalOutput").ap()
    gnn_program(nc, **args, spare=min(tile_pad // P, EIGHT))
    return run(nc, [feeds], core_ids=[0]).results[0]["out_0"]
```
